# Optimizing a Trainium2 kernel written in Bass

```python
import numpy as np
import jax
import jax.numpy as jnp

def _softmax(x, axis=-1):
    return jax.nn.softmax(x, axis=axis)

def _gelu(x):
    return jax.nn.gelu(x, approximate=True)

def _silu(x):
    return jax.nn.silu(x)

def _sigmoid(x):
    return jax.nn.sigmoid(x)

def _layernorm(x, axis=-1, eps=1e-05):
    m = jnp.mean(x, axis=axis, keepdims=True)
    v = jnp.var(x, axis=axis, keepdims=True)
    return (x - m) / jnp.sqrt(v + eps)

def _scatter_add(tgt, idx, src, axis=0):
    return tgt.at[idx].add(src)

def _segment_sum(src, seg, n):
    return jax.ops.segment_sum(src, seg, n)
kernel_name = 'mk_xattn_ffn_d2_seqx_r8_34d2ea'

def setup_inputs(seed: int=0):
    np.random.seed(seed)
    _w = jnp.asarray

    def _rec_inputs():
        import jax
        import jax.numpy as jnp
        _rk = jax.random.key(seed)
        x = 7.22e-05 + 1 * jax.random.normal(jax.random.fold_in(_rk, 1), (4, 512, 128), jnp.float32)
        _lenS = 512 - jax.random.randint(jax.random.fold_in(_rk, 7), (4,), 0, max(1, 512 // 4) + 1, jnp.int32)
        _lenS2 = 77 - jax.random.randint(jax.random.fold_in(_rk, 8), (4,), 0, max(1, 77 // 4) + 1, jnp.int32)
        _ctx_1024P = jax.random.normal(jax.random.fold_in(_rk, 11), (4, 16, 128), jnp.float32)
        _ctx_1024c = jax.random.dirichlet(jax.random.fold_in(_rk, 511), 0.3 * jnp.ones((16,), jnp.float32), (4, 77))
        _ctx_1024t = jnp.einsum('bsk,bkd->bsd', _ctx_1024c, _ctx_1024P)
        _ctx_1024t = _ctx_1024t * jax.lax.rsqrt(jnp.mean(jnp.square(_ctx_1024t)) + 1e-12) * 0.953939
        ctx_1024 = 4.13588e-05 + 0.999923 * (_ctx_1024t + 0.3 * jax.random.normal(jax.random.fold_in(_rk, 611), (4, 77, 128), jnp.float32))
        return (x, ctx_1024)
    x, ctx_1024 = _rec_inputs()

    def _L0_xattn_setup():
        import jax, jax.numpy as jnp
        import numpy as np
        D_MODEL = 128
        N_HEAD = 16
        D_HEAD = D_MODEL // N_HEAD
        key = jax.random.key(seed)
        ks = jax.random.split(key, 11)
        B, S = (2, 512)
        scale = 1.0 / np.sqrt(D_MODEL)
        inp = {'q': jax.random.normal(ks[0], (B, S, D_MODEL), jnp.float32), 'k': jax.random.normal(ks[1], (B, S, D_MODEL), jnp.float32), 'v': jax.random.normal(ks[2], (B, S, D_MODEL), jnp.float32), 'w_q': jax.random.normal(ks[3], (D_MODEL, D_MODEL), jnp.float32) * scale, 'b_q': jnp.zeros((D_MODEL,), jnp.float32), 'w_k': jax.random.normal(ks[4], (D_MODEL, D_MODEL), jnp.float32) * scale, 'b_k': jnp.zeros((D_MODEL,), jnp.float32), 'w_v': jax.random.normal(ks[5], (D_MODEL, D_MODEL), jnp.float32) * scale, 'b_v': jnp.zeros((D_MODEL,), jnp.float32), 'w_o': jax.random.normal(ks[6], (D_MODEL, D_MODEL), jnp.float32) * scale, 'b_o': jnp.zeros((D_MODEL,), jnp.float32)}
        return inp
    _L0_xattn_all = _L0_xattn_setup()
    _L0_xattn_in = {k: v for k, v in _L0_xattn_all.items() if k in ('w_q', 'b_q', 'w_k', 'b_k', 'w_v', 'b_v', 'w_o', 'b_o')}
    del _L0_xattn_all

    def _L0_ffn_setup():
        import jax, jax.numpy as jnp
        import numpy as np
        EPS = 1e-05

        def act_quant(x):
            scale = 127.0 / jnp.clip(jnp.max(jnp.abs(x), axis=-1, keepdims=True), EPS, None)
            q = jnp.clip(jnp.round(x * scale), -128.0, 127.0) / scale
            return x + jax.lax.stop_gradient(q - x)

        def weight_quant(w):
            scale = 1.0 / jnp.clip(jnp.mean(jnp.abs(w)), EPS, None)
            q = jnp.clip(jnp.round(w * scale), -1.0, 1.0) / scale
            return w + jax.lax.stop_gradient(q - w)

        def bitlinear(x, w):
            return act_quant(x) @ weight_quant(w).T
        key = jax.random.key(seed)
        k1, k2, k3, k4 = jax.random.split(key, 4)
        H, I = (128, 512)
        B, S = (4, 512)
        init = 0.02
        x = jax.random.normal(k1, (B, S, H), dtype=jnp.float32)
        w_gate = jax.random.normal(k2, (I, H), dtype=jnp.float32) * init
        w_up = jax.random.normal(k3, (I, H), dtype=jnp.float32) * init
        w_down = jax.random.normal(k4, (H, I), dtype=jnp.float32) * init
        return {'x': x, 'w_gate': w_gate, 'w_up': w_up, 'w_down': w_down}
    _L0_ffn_all = _L0_ffn_setup()
    _L0_ffn_in = {k: v for k, v in _L0_ffn_all.items() if k in ('w_gate', 'w_up', 'w_down')}
    del _L0_ffn_all

    def _L1_xattn_setup():
        import jax, jax.numpy as jnp
        import numpy as np
        import math
        D_MODEL = 128
        N_HEADS = 16
        HEAD_DIM = D_MODEL // N_HEADS
        TOP_K = 32
        SCALE = math.sqrt(HEAD_DIM)

        def _split_heads(t, n):
            B, L, _ = t.shape
            return t.reshape(B, L, N_HEADS, HEAD_DIM).transpose(0, 2, 1, 3)
        key = jax.random.key(seed)
        ks = jax.random.split(key, 12)
        B, S, N = (2, 256, 256)
        std = 1.0 / math.sqrt(D_MODEL)
        inp = {'x': jax.random.normal(ks[0], (B, S, D_MODEL), dtype=jnp.float32), 'knowledge_embeddings': jax.random.normal(ks[1], (B, N, D_MODEL), dtype=jnp.float32), 'Wq': jax.random.normal(ks[2], (D_MODEL, D_MODEL), dtype=jnp.float32) * std, 'bq': jnp.zeros((D_MODEL,), dtype=jnp.float32), 'Wk': jax.random.normal(ks[3], (D_MODEL, D_MODEL), dtype=jnp.float32) * std, 'bk': jnp.zeros((D_MODEL,), dtype=jnp.float32), 'Wv': jax.random.normal(ks[4], (D_MODEL, D_MODEL), dtype=jnp.float32) * std, 'bv': jnp.zeros((D_MODEL,), dtype=jnp.float32), 'Wo': jax.random.normal(ks[5], (D_MODEL, D_MODEL), dtype=jnp.float32) * std, 'bo': jnp.zeros((D_MODEL,), dtype=jnp.float32)}
        return inp
    _L1_xattn_all = _L1_xattn_setup()
    _L1_xattn_in = {k: v for k, v in _L1_xattn_all.items() if k in ('Wq', 'bq', 'Wk', 'bk', 'Wv', 'bv', 'Wo', 'bo')}
    del _L1_xattn_all

    def _L1_ffn_setup():
        import jax, jax.numpy as jnp
        import numpy as np
        BITS = 8
        LORA_RANK = 16
        LORA_ALPHA = 32
        SCALING = LORA_ALPHA / LORA_RANK

        def fake_quant_weight(w, bits=BITS):
            qmax = 2.0 ** (bits - 1) - 1
            scale = jnp.max(jnp.abs(w)) / qmax
            wq = jnp.clip(jnp.round(w / scale), -qmax - 1, qmax) * scale
            return w + jax.lax.stop_gradient(wq - w)

        def qat_lora_linear(x, W, b, A, B):
            Wq = fake_quant_weight(W)
            base = jnp.einsum('bsi,oi->bso', x, Wq) + b
            lora = jnp.einsum('bsr,or->bso', jnp.einsum('bsi,ri->bsr', x, A), B)
            return base + SCALING * lora
        key = jax.random.key(seed)
        ks = jax.random.split(key, 9)
        d, f = (128, 512)
        s_in = 1.0 / np.sqrt(d)
        s_ff = 1.0 / np.sqrt(f)
        return {'hidden_states': jax.random.normal(ks[0], (4, 256, d), jnp.float32), 'W_fc': jax.random.normal(ks[1], (f, d), jnp.float32) * s_in, 'b_fc': jnp.zeros((f,), jnp.float32), 'A_fc': jax.random.normal(ks[2], (LORA_RANK, d), jnp.float32) * s_in, 'B_fc': jnp.zeros((f, LORA_RANK), jnp.float32), 'W_proj': jax.random.normal(ks[3], (d, f), jnp.float32) * s_ff, 'b_proj': jnp.zeros((d,), jnp.float32), 'A_proj': jax.random.normal(ks[4], (LORA_RANK, f), jnp.float32) * s_ff, 'B_proj': jnp.zeros((d, LORA_RANK), jnp.float32)}
    _L1_ffn_all = _L1_ffn_setup()
    _L1_ffn_in = {k: v for k, v in _L1_ffn_all.items() if k in ('W_fc', 'b_fc', 'A_fc', 'B_fc', 'W_proj', 'b_proj', 'A_proj', 'B_proj')}
    del _L1_ffn_all
    return {'x': x, 'ctx_1024': ctx_1024, 'L0_xattn_w_q': _L0_xattn_in['w_q'], 'L0_xattn_b_q': _L0_xattn_in['b_q'], 'L0_xattn_w_k': _L0_xattn_in['w_k'], 'L0_xattn_b_k': _L0_xattn_in['b_k'], 'L0_xattn_w_v': _L0_xattn_in['w_v'], 'L0_xattn_b_v': _L0_xattn_in['b_v'], 'L0_xattn_w_o': _L0_xattn_in['w_o'], 'L0_xattn_b_o': _L0_xattn_in['b_o'], 'L0_ffn_w_gate': _L0_ffn_in['w_gate'], 'L0_ffn_w_up': _L0_ffn_in['w_up'], 'L0_ffn_w_down': _L0_ffn_in['w_down'], 'L1_xattn_Wq': _L1_xattn_in['Wq'], 'L1_xattn_bq': _L1_xattn_in['bq'], 'L1_xattn_Wk': _L1_xattn_in['Wk'], 'L1_xattn_bk': _L1_xattn_in['bk'], 'L1_xattn_Wv': _L1_xattn_in['Wv'], 'L1_xattn_bv': _L1_xattn_in['bv'], 'L1_xattn_Wo': _L1_xattn_in['Wo'], 'L1_xattn_bo': _L1_xattn_in['bo'], 'L1_ffn_W_fc': _L1_ffn_in['W_fc'], 'L1_ffn_b_fc': _L1_ffn_in['b_fc'], 'L1_ffn_A_fc': _L1_ffn_in['A_fc'], 'L1_ffn_B_fc': _L1_ffn_in['B_fc'], 'L1_ffn_W_proj': _L1_ffn_in['W_proj'], 'L1_ffn_b_proj': _L1_ffn_in['b_proj'], 'L1_ffn_A_proj': _L1_ffn_in['A_proj'], 'L1_ffn_B_proj': _L1_ffn_in['B_proj']}

def reference(x, ctx_1024, L0_xattn_w_q, L0_xattn_b_q, L0_xattn_w_k, L0_xattn_b_k, L0_xattn_w_v, L0_xattn_b_v, L0_xattn_w_o, L0_xattn_b_o, L0_ffn_w_gate, L0_ffn_w_up, L0_ffn_w_down, L1_xattn_Wq, L1_xattn_bq, L1_xattn_Wk, L1_xattn_bk, L1_xattn_Wv, L1_xattn_bv, L1_xattn_Wo, L1_xattn_bo, L1_ffn_W_fc, L1_ffn_b_fc, L1_ffn_A_fc, L1_ffn_B_fc, L1_ffn_W_proj, L1_ffn_b_proj, L1_ffn_A_proj, L1_ffn_B_proj):
    import jax
    import jax.numpy as jnp

    def _L0_xattn_ref(q, k, v, w_q, b_q, w_k, b_k, w_v, b_v, w_o, b_o):
        import jax, jax.numpy as jnp
        import numpy as np
        D_MODEL = 128
        N_HEAD = 16
        D_HEAD = D_MODEL // N_HEAD
        B, S, _ = q.shape

        def proj(x, w, b):
            y = x @ w.T + b
            return y.reshape(B, -1, N_HEAD, D_HEAD).transpose(0, 2, 1, 3)
        query = proj(q, w_q, b_q)
        key_ = proj(k, w_k, b_k)
        value = proj(v, w_v, b_v)
        scores = jnp.einsum('bhsd,bhtd->bhst', query, key_) / jnp.sqrt(jnp.asarray(D_HEAD, query.dtype))
        attn = jax.nn.softmax(scores, axis=-1)
        out = jnp.einsum('bhst,bhtd->bhsd', attn, value)
        out = out.transpose(0, 2, 1, 3).reshape(B, S, D_MODEL)
        return out @ w_o.T + b_o

    def _L0_ffn_ref(x, w_gate, w_up, w_down):
        import jax, jax.numpy as jnp
        import numpy as np
        EPS = 1e-05

        def act_quant(x):
            scale = 127.0 / jnp.clip(jnp.max(jnp.abs(x), axis=-1, keepdims=True), EPS, None)
            q = jnp.clip(jnp.round(x * scale), -128.0, 127.0) / scale
            return x + jax.lax.stop_gradient(q - x)

        def weight_quant(w):
            scale = 1.0 / jnp.clip(jnp.mean(jnp.abs(w)), EPS, None)
            q = jnp.clip(jnp.round(w * scale), -1.0, 1.0) / scale
            return w + jax.lax.stop_gradient(q - w)

        def bitlinear(x, w):
            return act_quant(x) @ weight_quant(w).T
        g = bitlinear(x, w_gate)
        u = bitlinear(x, w_up)
        h = jnp.square(jax.nn.relu(g)) * u
        return bitlinear(h, w_down)

    def _L1_xattn_ref(x, knowledge_embeddings, Wq, bq, Wk, bk, Wv, bv, Wo, bo):
        import jax, jax.numpy as jnp
        import numpy as np
        import math
        D_MODEL = 128
        N_HEADS = 16
        HEAD_DIM = D_MODEL // N_HEADS
        TOP_K = 32
        SCALE = math.sqrt(HEAD_DIM)

        def _split_heads(t, n):
            B, L, _ = t.shape
            return t.reshape(B, L, N_HEADS, HEAD_DIM).transpose(0, 2, 1, 3)
        B, S, _ = x.shape
        N = knowledge_embeddings.shape[1]
        Q = _split_heads(x @ Wq.T + bq, N_HEADS)
        K = _split_heads(knowledge_embeddings @ Wk.T + bk, N_HEADS)
        V = _split_heads(knowledge_embeddings @ Wv.T + bv, N_HEADS)
        scores = jnp.einsum('bhsd,bhnd->bhsn', Q, K) / SCALE
        k = min(TOP_K, N)
        topk_scores, topk_indices = jax.lax.top_k(scores, k)
        sparse_weights = jax.nn.softmax(topk_scores, axis=-1)
        sel_V = jnp.take_along_axis(V[:, :, None, :, :], topk_indices[..., None], axis=3)
        context = jnp.einsum('bhsk,bhskd->bhsd', sparse_weights, sel_V)
        context = context.transpose(0, 2, 1, 3).reshape(B, S, D_MODEL)
        return context @ Wo.T + bo

    def _L1_ffn_ref(hidden_states, W_fc, b_fc, A_fc, B_fc, W_proj, b_proj, A_proj, B_proj):
        import jax, jax.numpy as jnp
        import numpy as np
        BITS = 8
        LORA_RANK = 16
        LORA_ALPHA = 32
        SCALING = LORA_ALPHA / LORA_RANK

        def fake_quant_weight(w, bits=BITS):
            qmax = 2.0 ** (bits - 1) - 1
            scale = jnp.max(jnp.abs(w)) / qmax
            wq = jnp.clip(jnp.round(w / scale), -qmax - 1, qmax) * scale
            return w + jax.lax.stop_gradient(wq - w)

        def qat_lora_linear(x, W, b, A, B):
            Wq = fake_quant_weight(W)
            base = jnp.einsum('bsi,oi->bso', x, Wq) + b
            lora = jnp.einsum('bsr,or->bso', jnp.einsum('bsi,ri->bsr', x, A), B)
            return base + SCALING * lora
        h = qat_lora_linear(hidden_states, W_fc, b_fc, A_fc, B_fc)
        h = jax.nn.gelu(h, approximate=False)
        h = qat_lora_linear(h, W_proj, b_proj, A_proj, B_proj)
        return h
    x = x + _L0_xattn_ref(_layernorm(x, axis=-1), ctx_1024, ctx_1024, L0_xattn_w_q, L0_xattn_b_q, L0_xattn_w_k, L0_xattn_b_k, L0_xattn_w_v, L0_xattn_b_v, L0_xattn_w_o, L0_xattn_b_o)
    x = x + _L0_ffn_ref(_layernorm(x, axis=-1), L0_ffn_w_gate, L0_ffn_w_up, L0_ffn_w_down)
    x = x + _L1_xattn_ref(_layernorm(x, axis=-1), ctx_1024, L1_xattn_Wq, L1_xattn_bq, L1_xattn_Wk, L1_xattn_bk, L1_xattn_Wv, L1_xattn_bv, L1_xattn_Wo, L1_xattn_bo)
    x = x + _L1_ffn_ref(_layernorm(x, axis=-1), L1_ffn_W_fc, L1_ffn_b_fc, L1_ffn_A_fc, L1_ffn_B_fc, L1_ffn_W_proj, L1_ffn_b_proj, L1_ffn_A_proj, L1_ffn_B_proj)
    return x

_drawn_inputs = setup_inputs


def setup_inputs(seed=0):
    import zlib

    import numpy as np

    out = dict(_drawn_inputs(seed))
    spreads = {'L0_xattn_b_q': (0.0, 0.35),
     'L0_xattn_b_k': (0.0, 2.0),
     'L0_xattn_b_v': (0.0, 0.1),
     'L0_xattn_b_o': (0.0, 0.1),
     'L1_xattn_bq': (0.0, 0.8),
     'L1_xattn_bk': (0.0, 2.0),
     'L1_xattn_bv': (0.0, 0.751),
     'L1_xattn_bo': (0.0, 0.753),
     'L1_ffn_b_fc': (0.0, 0.8),
     'L1_ffn_B_fc': (0.0, 0.1),
     'L1_ffn_b_proj': (0.0, 0.722),
     'L1_ffn_B_proj': (0.0, 0.1)}
    factors = {'L0_ffn_w_gate': 8.0, 'L0_ffn_w_up': 8.0, 'L0_ffn_w_down': 8.0}
    for name, (base, spread) in spreads.items():
        noise = np.random.default_rng([zlib.crc32(name.encode()), seed]).standard_normal(out[name].shape)
        drawn = base * np.exp(spread * noise) if base else spread * noise
        out[name] = jnp.asarray(drawn.astype(out[name].dtype))
    for name, factor in factors.items():
        out[name] = (out[name] * factor).astype(out[name].dtype)
    return out
```

```python
from contextlib import ExitStack

import concourse.bass as bass
from concourse import mybir

F32 = mybir.dt.float32
BF16 = mybir.dt.bfloat16
ALU = mybir.AluOpType
ACT = mybir.ActivationFunctionType
X = mybir.AxisListType.X
RMAX = bass.bass_isa.ReduceOp.max
RADD = bass.bass_isa.ReduceOp.add

B, S, D = 4, 512, 128
CTX = 77
H = 16
DH = D // H
FF = 512
FC = FF // D
RANK = 16
P = 128
TILES = B * S // P
TPB = S // P
HC = 4
NCH = H // HC
SC = HC * CTX
HJ = H * CTX
VW = DH + 1
ROUNDS = 4
LN_EPS = 1e-5
Q_EPS = 1e-5
LORA_SCALE = 2.0
ROUND = 12582912.0
TAKEN = -float(2 ** 120)
ISQ = float(DH) ** -0.5

PA = {}
PB = {}
PC = {}
ROW = {}
R16 = {}


def _lay(table, *parts):
    at = 0
    for name, width in parts:
        table[name] = (at, at + width)
        at += width
    return at


PA_W = _lay(PA, ("ident", P), ("hmask", H), ("bq0", 1), ("bk0", 1), ("wq0", D), ("wk0", D), ("wv0", D), ("wo0", D),
            ("ctx", B * CTX))
PB_W = _lay(PB, ("gate", FF), ("up", FF), ("down", FF))
PC_W = _lay(PC, ("wq1", D), ("wk1", D), ("wv1", D), ("wo1", D), ("bq1", 1), ("bk1", 1), ("bfc", FC), ("fc", FF),
            ("proj", FF))
ROW_W = _lay(ROW, ("bv0", D), ("bo0", D), ("bv1", D), ("bo1", D), ("bproj", D))
R16_W = _lay(R16, ("afc", D), ("bfcT", FF), ("aproj", FF), ("bprojT", D))

FIRST, LAST = -2, TILES + 1
LOOP = (2, 3)
LOOPS = (TILES - 4) // 2


def has(stage, c):
    if stage == "G":
        return c % 2 == 1 and 3 <= c <= LAST
    tile = c + {"A": 2, "F": 1, "T": 0, "C": -1}[stage]
    return 0 <= tile < TILES


class Step:

    def __init__(self, c, j=None):
        self.c, self.j = c, j

    def has(self, stage):
        return has(stage, self.c)

    def plus(self, fixed, per_pair):
        return fixed if self.j is None or per_pair == 0 else self.j * per_pair + fixed

    def done(self, tile, per_tile=1, more=0):
        return self.plus(per_tile * tile + more, 2 * per_tile)

    def loaded(self, tile):
        return self.plus(16 * (tile // 2 + 1), 16)

    def pairs(self, g, per_pair=1, more=0):
        return self.plus(per_pair * g + more, per_pair)

    def batch(self, tile):
        if self.j is None:
            return tile // TPB
        return (self.j + tile // 2) // (TPB // 2)


def standing_for(c):
    return LOOP[c % 2] if LOOP[0] <= c < LOOP[0] + 2 * LOOPS else c


ORDER = ["setup0", -2, "setup1", -1] + list(range(0, LAST + 1))


class Bank:

    def __init__(self, tensors, full, out, setup0, setup1, names):
        self.tensors, self.full, self.out = tensors, full, out
        self.fixed = {"setup0": setup0, "setup1": setup1}
        self.names = names

    def users(self, key):
        if key in self.fixed:
            return self.fixed[key]
        return [n for n in self.names if has(n[0].upper(), key)]

    def turn(self, step, name, back=0):
        key = step.c if not back else step.c - back
        before = sum(len(self.users(k)) for k in ORDER[:ORDER.index(key)])
        return before + self.users(key).index(name), sum(len(self.users(k)) for k in LOOP)

    def slot(self, step, name):
        n, per_pair = self.turn(step, name)
        assert step.j is None or per_pair % len(self.tensors) == 0
        return self.tensors[n % len(self.tensors)]

    def take(self, pe, step, name):
        n, per_pair = self.turn(step, name)
        n -= len(self.tensors) - 1
        if n > 0:
            pe.wait_ge(self.out, step.plus(n, per_pair))
        return self.slot(step, name)

    def see(self, eng, step, name):
        n, per_pair = self.turn(step, name)
        eng.wait_ge(self.full, step.plus(n + 1, per_pair))
        return self.slot(step, name)

    def landed(self, eng, step, name, back=0):
        n, per_pair = self.turn(step, name, back)
        eng.wait_ge(self.out, step.plus(n + 1, per_pair))

    def used(self, eng, step, name, back=0):
        n, per_pair = self.turn(step, name, back)
        eng.wait_ge(self.full, step.plus(n + 1, per_pair))


def build(nc, x, pa, pb, pc, rows, r16, out):
    with ExitStack() as ctx:
        def sb(name, shape, dt=F32):
            return ctx.enter_context(nc.sbuf_tensor(name, shape, dt))

        def sem(name):
            return ctx.enter_context(nc.semaphore(name))

        pa_s, pb_s, pc_s = sb("pa_s", [P, PA_W]), sb("pb_s", [P, PB_W]), sb("pc_s", [P, PC_W])
        row_s, r16_s = sb("row_s", [1, ROW_W]), sb("r16_s", [RANK, R16_W])

        def part(name):
            for tensor, table in ((pa_s, PA), (pb_s, PB), (pc_s, PC), (row_s, ROW), (r16_s, R16)):
                if name in table:
                    return tensor[:, table[name][0]:table[name][1]]

        ident = part("ident")
        ones = sb("ones", [1, P])
        eps, mhalf = sb("eps", [P, 1]), sb("mhalf", [P, 1])
        wsum = sb("wsum", [P, 8])
        wtot = sb("wtot", [P, 8])
        wscale = sb("wscale", [P, 8])
        wrec = sb("wrec", [P, 8])
        wcub = sb("wcub", [P, 2])
        wtmp = sb("wtmp", [P, 2, FF])
        gateQ, upQ, downQ = (sb(n, [P, FF], BF16) for n in ("gateQ", "upQ", "downQ"))
        fcW, projW = sb("fcW", [P, FF]), sb("projW", [P, FF])
        KT = [sb(f"KT{l}", [P, B * CTX]) for l in range(2)]
        KB = [sb(f"KB{l}", [P, B * HJ]) for l in range(2)]
        V = [sb(f"V{l}", [CTX, B * H * VW]) for l in range(2)]

        xin = sb("xin", [P, 2, D])
        stats = {k: sb(f"stats_{k}", [P, 2, 6]) for k in "afdc"}
        mv = {k: sb(f"mv_{k}", [P, 2, 2]) for k in "afdc"}
        ve = {k: sb(f"ve_{k}", [P, 1]) for k in "afdc"}
        rstd = {k: sb(f"rstd_{k}", [P, 2]) for k in "afdc"}
        cen = {k: sb(f"cen_{k}", [P, 2, D]) for k in "afdc"}
        xn = {k: sb(f"xn_{k}", [P, D]) for k in "adc"}
        xT = {k: sb(f"xT_{k}", [P, P]) for k in "ad"}
        qT = {k: sb(f"qT_{k}", [P, P]) for k in "ad"}
        s0, e0 = sb("s0", [P, HJ]), sb("e0", [P, HJ])
        nmax = sb("nmax", [P, 2, H])
        pT = {k: sb(f"pT_{k}", [CTX, H * P]) for k in "ac"}
        osb = {k: sb(f"osb_{k}", [P, H * VW]) for k in "ac"}
        rden = {k: sb(f"rden_{k}", [P, 2, H]) for k in "ac"}
        on = {k: sb(f"on_{k}", [P, D]) for k in "ac"}
        oT = {k: sb(f"oT_{k}", [P, P]) for k in "ac"}
        x1, x2, x2keep, x3 = (sb(n, [P, 2, D]) for n in ("x1", "x2", "x2keep", "x3"))
        amax = sb("amax", [P, 2, 4])
        actA = sb("actA", [P, 2])
        yq, yqT = sb("yq", [P, P]), sb("yqT", [P, P], BF16)
        cub = sb("cub", [P, 3])
        relu_g, up_s, prod, hid = (sb(n, [P, FF]) for n in ("relu_g", "up_s", "prod", "hid"))
        hmax = sb("hmax", [P, 2, 4])
        hA, osc = sb("hA", [P, 2]), sb("osc", [P, 2])
        hq, hqT = sb("hq", [P, FF]), sb("hqT", [P, FF], BF16)
        s1 = [sb(f"s1_{i}", [P, HJ]) for i in range(2)]
        rest = [sb(f"rest_{i}", [P, HJ]) for i in range(2)]
        top = sb("top", [P, 2, H, ROUNDS, 8])
        sm1, e1, mask, p1 = (sb(n, [P, HJ]) for n in ("sm1", "e1", "mask", "p1"))
        x4T = sb("x4T", [P, 2, P])
        hT = sb("hT", [P, FC, 2 * P])
        y = sb("y", [P, 2, D])
        mark = sb("mark", [1, 2])

        pa_in, pb_in, pc_in, row_in, r16_in = (sem(n) for n in ("pa_in", "pb_in", "pc_in", "row_in", "r16_in"))
        consts_set, kb_ready = sem("consts_set"), sem("kb_ready")
        w_summed, w_totalled, w_chain, w_ready = (sem(n) for n in ("w_summed", "w_totalled", "w_chain", "w_ready"))
        x_in, x2_kept = [sem("x_in_even"), sem("x_in_odd")], [sem("x2_kept_even"), sem("x2_kept_odd")]
        y_stored = sem("y_stored")
        gate = sem("gate")
        dve_step = [sem("dve_step_even"), sem("dve_step_odd")]
        dve_over, dve_cleared = sem("dve_over"), sem("dve_cleared")
        ln = {k: {n: sem(f"{k}_{n}") for n in ("stats", "chain", "centred", "normed")} for k in "afdc"}
        nmax_ready, s0_shifted, e0_ready = sem("nmax_ready"), sem("s0_shifted"), sem("e0_ready")
        rden_ready = {k: sem(f"rden_ready_{k}") for k in "ac"}
        on_ready = {k: sem(f"on_ready_{k}") for k in "ac"}
        actA_ready, yq_ready, cub_chain, cub_ready = (sem(n) for n in ("actA_ready", "yq_ready", "cub_chain", "cub_ready"))
        prod_ready, hid_ready, hA_ready, hq_ready = (sem(n) for n in ("prod_ready", "hid_ready", "hA_ready", "hq_ready"))
        top_ready, sm1_ready, e1_ready, mask_ready, p1_ready = (
            sem(n) for n in ("top_ready", "sm1_ready", "e1_ready", "mask_ready", "p1_ready"))

        banks = [ctx.enter_context(nc.psum_tensor(f"bank{i}", [P, 512], F32)) for i in range(8)]

        def bank(name, tensors, setup0, setup1, names):
            return Bank(tensors, sem(f"{name}_full"), sem(f"{name}_out"), setup0, setup1, names)

        m = bank("m", [banks[0]], [], [],
                 ["a_xT", "f_yT", "a_q", "f_xT", "f_q", "a_oT", "a_out", "c_oT", "c_out", "c_xT"])
        o = bank("o", [banks[1]], [], [], ["a_o", "c_o"])
        g = bank("g", [banks[2]], [], ["lora_fc"], ["g_h0", "f_g", "f_hT"])
        u = bank("u", [banks[3]], [], ["lora_proj"], ["g_h1", "g_out", "f_u", "f_down"])
        s = bank("s", banks[4:6], ["keys0"], ["keys1"], [f"{k}_s{i}" for k in "af" for i in range(NCH)])
        t = bank("t", banks[6:8], ["v0"], ["v1"], [f"{k}_t{i}" for k in "ac" for i in range(NCH)])
        setup0, setup1 = Step("setup0"), Step("setup1")

        def heads(ap, w=CTX):
            return ap.rearrange("p (h j) -> p h j", j=w)

        def middle_and_end(eng, step_):
            for c in range(1, LOOP[0]):
                step_(Step(c))
            with eng.Fori(0, LOOPS) as j:
                for c in LOOP:
                    step_(Step(c, j))
            for c in range(LOOP[0] + 2 * LOOPS, LAST + 1):
                step_(Step(c))

        block = ctx.enter_context(nc.Block())
        dve_counts = {}

        @block.vector
        def _(dve):
            dve.memset(ones[:, :], 1.0).then_inc(consts_set, 1)
            for l in range(2):
                dve.memset(V[l][:, :], 1.0).then_inc(consts_set, 1)
            dve.memset(eps[:, :], LN_EPS).then_inc(consts_set, 1)
            dve.memset(mhalf[:, :], -0.5).then_inc(consts_set, 1)

            class Own:

                def __init__(self, step):
                    self.sem, self.n = dve_step[step.c % 2], 0

                def out(self, ins):
                    self.n += 1
                    ins.then_inc(self.sem, 1)
                    return self.n

                def wait(self, n):
                    dve.wait_ge(self.sem, n)

            def ln_stats(own, step, k, src, tile):
                par = tile % 2
                if tile >= 2:
                    dve.wait_ge(ln[k]["normed"], step.done(tile - 1))
                n = own.out(dve.bn_stats(stats[k][:, par, :], src))
                own.wait(n)
                dve.bn_aggr(mv[k][:, par, :], stats[k][:, par, :]).then_inc(ln[k]["stats"], 1)

            def a_stats(own, step):
                a = step.c + 2
                dve.wait_ge(x_in[a % 2], step.loaded(a))
                ln_stats(own, step, "a", xin[:, a % 2, :], a)

            def a_max(own, step):
                a = step.c + 2
                s.landed(dve, step, f"a_s{NCH - 1}")
                dve.tensor_reduce(nmax[:, a % 2, :], heads(s0[:, :]), X, ALU.max, negate=True).then_inc(nmax_ready, 1)

            def recip(step, k, tile):
                o.landed(dve, step, f"{k}_o")
                dve.reciprocal(rden[k][:, tile % 2, :], heads(osb[k][:, :], VW)[:, :, DH]).then_inc(rden_ready[k], 1)

            def f_stats(own, step):
                f = step.c + 1
                m.landed(dve, step, "a_out", back=1)
                ln_stats(own, step, "f", x1[:, f % 2, :], f)

            def f_scale(own, step):
                f = step.c + 1
                par = f % 2
                a_ = amax[:, par, :]
                dve.wait_ge(ln["f"]["centred"], step.done(f + 1))
                n = own.out(dve.tensor_reduce(a_[:, 0:1], cen["f"][:, par, :], X, ALU.max, apply_absolute_value=True))
                dve.wait_ge(ln["f"]["normed"], step.done(f + 1))
                own.wait(n)
                n = own.out(dve.tensor_tensor(a_[:, 1:2], a_[:, 0:1], rstd["f"][:, par:par + 1], ALU.mult))
                own.wait(n)
                n = own.out(dve.tensor_scalar(a_[:, 2:3], a_[:, 1:2], Q_EPS, 1.0 / 127.0, ALU.max, ALU.mult))
                own.wait(n)
                n = own.out(dve.reciprocal(a_[:, 3:4], a_[:, 2:3]))
                own.wait(n)
                dve.tensor_tensor(actA[:, par:par + 1], a_[:, 3:4], rstd["f"][:, par:par + 1], ALU.mult)\
                   .then_inc(actA_ready, 1)

            def f_hidden_scale(own, step):
                f = step.c + 1
                par = f % 2
                h_ = hmax[:, par, :]
                dve.wait_ge(hid_ready, step.done(f + 1))
                n = own.out(dve.tensor_reduce(h_[:, 0:1], hid[:, :], X, ALU.max, apply_absolute_value=True))
                dve.wait_ge(cub_ready, step.done(f + 1))
                own.wait(n)
                n = own.out(dve.tensor_tensor(h_[:, 1:2], h_[:, 0:1], cub[:, 2:3], ALU.mult))
                own.wait(n)
                n = own.out(dve.tensor_scalar(h_[:, 2:3], h_[:, 1:2], Q_EPS, 1.0 / 127.0, ALU.max, ALU.mult))
                own.wait(n)
                osc_made = own.out(dve.tensor_tensor(osc[:, par:par + 1], h_[:, 2:3], wscale[:, 2:3], ALU.mult))
                n = own.out(dve.reciprocal(h_[:, 3:4], h_[:, 2:3]))
                own.wait(n)
                dve.tensor_tensor(hA[:, par:par + 1], h_[:, 3:4], cub[:, 2:3], ALU.mult).then_inc(hA_ready, 1)
                return osc_made

            def f_residual(own, step, osc_made):
                f = step.c + 1
                par = f % 2
                product = u.see(dve, step, "f_down")
                if f >= 2:
                    dve.wait_ge(x2_kept[par], step.loaded(f - 2))
                own.wait(osc_made)
                dve.scalar_tensor_tensor(x2[:, par, :], product[:, 0:D], osc[:, par:par + 1], x1[:, par, :],
                                         ALU.mult, ALU.add).then_inc(u.out, 1)
                u.landed(dve, step, "f_down")
                ln_stats(own, step, "d", x2[:, par, :], f)

            def c_stats(own, step):
                p = step.c - 1
                m.landed(dve, step, "c_out")
                ln_stats(own, step, "c", x3[:, p % 2, :], p)

            def top_rounds(own, step):
                par = step.c % 2
                scores, marked = heads(s1[par][:, :]), heads(rest[par][:, :])
                for h0 in range(0, H, 8):
                    made = {}
                    for r in range(ROUNDS):
                        src = marked if r else scores
                        for h in range(h0, h0 + 8):
                            if r:
                                own.wait(made[h])
                            made[h] = own.out(dve.max(top[:, par, h, r, :], src[:, h, :]))
                            yield
                        for h in range(h0, h0 + 8):
                            own.wait(made[h])
                            ins = dve.match_replace(marked[:, h, :], top[:, par, h, r, :], src[:, h, :], TAKEN)
                            if r == ROUNDS - 1:
                                ins.then_inc(top_ready, 1)
                            else:
                                made[h] = own.out(ins)
                            yield

            def step_(step):
                c = step.c
                own = Own(step)
                if c >= 0:
                    dve.wait_ge(dve_cleared, step.plus(c + 1, 2))
                    dve.sem_inc(gate, 1)
                if step.has("T"):
                    s.landed(dve, step, f"f_s{NCH - 1}", back=1)
                    dve.sem_inc(gate, 1)
                    if c >= 2:
                        dve.wait_ge(mask_ready, step.done(c - 1))
                        dve.sem_inc(gate, 1)
                        dve.wait_ge(sm1_ready, step.done(c - 1))
                        dve.sem_inc(gate, 1)
                small, kept = [], {}
                if step.has("A"):
                    small += [(DUE["a_stats"], lambda: a_stats(own, step)), (DUE["a_max"], lambda: a_max(own, step)),
                              (DUE["a_recip"], lambda: recip(step, "a", c + 2))]
                if step.has("F"):
                    small += [(DUE["f_stats"], lambda: f_stats(own, step)), (DUE["f_scale"], lambda: f_scale(own, step)),
                              (DUE["f_hidden"], lambda: kept.update(osc=f_hidden_scale(own, step))),
                              (DUE["f_residual"], lambda: f_residual(own, step, kept["osc"]))]
                if step.has("C"):
                    small += [(DUE["c_recip"], lambda: recip(step, "c", c - 1)), (DUE["c_stats"], lambda: c_stats(own, step))]
                small.sort(key=lambda due: due[0])
                if step.has("T"):
                    for n, _ in enumerate(top_rounds(own, step)):
                        while small and small[0][0] <= n:
                            small.pop(0)[1]()
                while small:
                    small.pop(0)[1]()
                dve.memset(mark[:, c % 2:c % 2 + 1], 0.0).then_inc(dve_over, 1)
                dve_counts[c] = own.n

            def block_keys(layer, b):
                dve.tensor_tensor(heads(KB[layer][:, b * HJ:(b + 1) * HJ]),
                                  KT[layer][:, b * CTX:(b + 1) * CTX].unsqueeze(1).to_broadcast([P, H, CTX]),
                                  part("hmask").unsqueeze(2).to_broadcast([P, H, CTX]), ALU.mult).then_inc(kb_ready, 1)

            def weight_scales():
                dve.wait_ge(pb_in, 16)
                for i, name in enumerate(("gate", "up", "down")):
                    dve.tensor_reduce(wsum[:, i:i + 1], part(name), X, ALU.add, apply_absolute_value=True)\
                       .then_inc(w_summed, 1)
                dve.wait_ge(pc_in, 16)
                for i, name in enumerate(("fc", "proj")):
                    dve.tensor_reduce(wsum[:, 3 + i:4 + i], part(name), X, ALU.max, apply_absolute_value=True)\
                       .then_inc(w_summed, 1)
                dve.wait_ge(w_totalled, 2)
                dve.tensor_scalar(wscale[:, 0:3], wtot[:, 0:3], 1.0 / (FF * D), Q_EPS, ALU.mult, ALU.max)\
                   .then_inc(w_chain, 1)
                dve.tensor_scalar(wscale[:, 3:5], wtot[:, 3:5], 1.0 / 127.0, None, ALU.mult).then_inc(w_chain, 1)
                dve.wait_ge(w_chain, 2)
                dve.reciprocal(wrec[:, 0:5], wscale[:, 0:5]).then_inc(w_chain, 1)
                dve.tensor_tensor(wcub[:, 0:1], wscale[:, 0:1], wscale[:, 0:1], ALU.mult).then_inc(w_chain, 1)
                dve.wait_ge(w_chain, 4)
                dve.tensor_tensor(wcub[:, 1:2], wcub[:, 0:1], wscale[:, 1:2], ALU.mult).then_inc(w_chain, 1)
                return 5

            def round_weights(chain):
                for i, (name, dst) in enumerate((("gate", gateQ), ("up", upQ), ("down", downQ))):
                    tmp = wtmp[:, i % 2, :]
                    if i == 2:
                        dve.wait_ge(w_ready, 1)
                    dve.tensor_scalar(tmp, part(name), wrec[:, i:i + 1], 1.0, ALU.mult, ALU.min).then_inc(w_chain, 1)
                    dve.wait_ge(w_chain, chain + 1)
                    dve.tensor_scalar(tmp, tmp, -1.0, ROUND, ALU.max, ALU.add).then_inc(w_chain, 1)
                    dve.wait_ge(w_chain, chain + 2)
                    dve.tensor_scalar(dst[:, :], tmp, -ROUND, None, ALU.add).then_inc(w_ready, 1)
                    chain += 2
                dve.wait_ge(w_ready, 3)
                for i, (name, where, user) in enumerate((("fc", g, "lora_fc"), ("proj", u, "lora_proj"))):
                    tmp = wtmp[:, i, :]
                    dve.tensor_scalar(tmp, part(name), wrec[:, 3 + i:4 + i], 127.0, ALU.mult, ALU.min)\
                       .then_inc(w_chain, 1)
                    dve.wait_ge(w_chain, chain + 1)
                    dve.tensor_scalar(tmp, tmp, -128.0, ROUND, ALU.max, ALU.add).then_inc(w_chain, 1)
                    dve.wait_ge(w_chain, chain + 2)
                    dve.tensor_scalar(tmp, tmp, -ROUND, wscale[:, 3 + i:4 + i], ALU.add, ALU.mult).then_inc(w_chain, 1)
                    chain += 3
                    product = where.see(dve, setup1, user)
                    dve.wait_ge(w_chain, chain)
                    dve.scalar_tensor_tensor((fcW, projW)[i][:, :], product[:, :], LORA_SCALE, tmp, ALU.mult, ALU.add)\
                       .then_inc(where.out, 1)

            dve.wait_ge(pa_in, 16)
            s.landed(dve, setup0, "keys0")
            block_keys(0, 0)
            step_(Step(-2))
            chain = weight_scales()
            round_weights(chain)
            s.landed(dve, setup1, "keys1")
            block_keys(1, 0)
            step_(Step(-1))
            step_(Step(0))
            middle_and_end(dve, step_)

        @block.gpsimd
        def _(pool):
            def norm(step, k, src, tile, turn=None, back=1):
                par = tile % 2
                pool.wait_ge(ln[k]["stats"], step.done(tile + 1))
                if k == "f" and tile >= 2:
                    pool.wait_ge(yq_ready, step.done(tile - 1))
                pool.tensor_tensor(cen[k][:, par, :], src, mv[k][:, par, 0:1].to_broadcast([P, D]), ALU.subtract)\
                    .then_inc(ln[k]["centred"], 1)
                pool.tensor_tensor(ve[k][:, :], mv[k][:, par, 1:2], eps[:, :], ALU.add).then_inc(ln[k]["chain"], 1)
                if turn is None:
                    pool.wait_ge(ln[k]["chain"], step.done(tile + 1))
                    pool.tensor_tensor(rstd[k][:, par:par + 1], ve[k][:, :], mhalf[:, :], ALU.pow)\
                        .then_inc(ln[k]["normed"], 1)
                    return
                pool.wait_ge(ln[k]["chain"], step.done(tile, 2, 1))
                pool.tensor_tensor(rstd[k][:, par:par + 1], ve[k][:, :], mhalf[:, :], ALU.pow)\
                    .then_inc(ln[k]["chain"], 1)
                pool.wait_ge(ln[k]["centred"], step.done(tile + 1))
                if tile >= 1:
                    m.used(pool, step, turn, back=1)
                pool.wait_ge(ln[k]["chain"], step.done(tile, 2, 2))
                pool.tensor_tensor(xn[k][:, :], cen[k][:, par, :], rstd[k][:, par:par + 1].to_broadcast([P, D]),
                                   ALU.mult).then_inc(ln[k]["normed"], 1)

            def heads_out(step, k, tile):
                pool.wait_ge(rden_ready[k], step.done(tile + 1))
                if tile >= 1:
                    m.used(pool, step, f"{k}_oT", back=1)
                pool.tensor_tensor(heads(on[k][:, :], DH), heads(osb[k][:, :], VW)[:, :, 0:DH],
                                   rden[k][:, tile % 2, :].unsqueeze(2).to_broadcast([P, H, DH]), ALU.mult)\
                    .then_inc(on_ready[k], 1)

            def step_(step):
                c = step.c
                a, f, p = c + 2, c + 1, c - 1
                if step.has("A"):
                    norm(step, "a", xin[:, a % 2, :], a, "a_xT")
                if step.has("F"):
                    norm(step, "f", x1[:, f % 2, :], f)
                if step.has("C"):
                    pool.wait_ge(top_ready, step.done(p + 1, H))
                    if p >= 1:
                        pool.wait_ge(e1_ready, step.done(p))
                    pool.tensor_tensor(heads(sm1[:, :]), heads(s1[p % 2][:, :]),
                                       top[:, p % 2, :, 0, 0:1].to_broadcast([P, H, CTX]), ALU.subtract)\
                        .then_inc(sm1_ready, 1)
                if step.has("F"):
                    pool.wait_ge(actA_ready, step.done(f + 1))
                    if f == 0:
                        pool.wait_ge(w_chain, 5)
                    if f >= 1:
                        pool.wait_ge(hA_ready, step.done(f))
                    scale = amax[:, f % 2, 2:3]
                    pool.tensor_tensor(cub[:, 0:1], scale, scale, ALU.mult).then_inc(cub_chain, 1)
                    pool.tensor_tensor(cub[:, 1:2], scale, wcub[:, 1:2], ALU.mult).then_inc(cub_chain, 1)
                    pool.wait_ge(cub_chain, step.done(f + 1, 2))
                    pool.tensor_tensor(cub[:, 2:3], cub[:, 0:1], cub[:, 1:2], ALU.mult).then_inc(cub_ready, 1)
                    g.landed(pool, step, "f_g")
                    u.landed(pool, step, "f_u")
                    pool.tensor_tensor(prod[:, :], relu_g[:, :], up_s[:, :], ALU.mult).then_inc(prod_ready, 1)
                    if f >= 1:
                        pool.wait_ge(hq_ready, step.done(f))
                    pool.wait_ge(prod_ready, step.done(f + 1))
                    pool.tensor_tensor(hid[:, :], prod[:, :], relu_g[:, :], ALU.mult).then_inc(hid_ready, 1)
                if step.has("A"):
                    pool.wait_ge(nmax_ready, step.done(a + 1))
                    if a >= 1:
                        t.used(pool, step, f"a_t{NCH - 1}", back=1)
                    pool.tensor_tensor(heads(e0[:, :]), heads(s0[:, :]),
                                       nmax[:, a % 2, :].unsqueeze(2).to_broadcast([P, H, CTX]), ALU.add)\
                        .then_inc(s0_shifted, 1)
                if step.has("C"):
                    pool.wait_ge(e1_ready, step.done(p + 1))
                    pool.wait_ge(mask_ready, step.done(p + 1))
                    if p >= 1:
                        t.used(pool, step, f"c_t{NCH - 1}", back=1)
                    pool.tensor_tensor(p1[:, :], e1[:, :], mask[:, :], ALU.mult).then_inc(p1_ready, 1)
                if step.has("F"):
                    norm(step, "d", x2[:, f % 2, :], f, "f_xT")
                if step.has("A"):
                    heads_out(step, "a", a)
                if step.has("C"):
                    heads_out(step, "c", p)
                    norm(step, "c", x3[:, p % 2, :], p, "c_xT")

            def block_keys(layer, b):
                pool.tensor_tensor(heads(KB[layer][:, b * HJ:(b + 1) * HJ]),
                                   KT[layer][:, b * CTX:(b + 1) * CTX].unsqueeze(1).to_broadcast([P, H, CTX]),
                                   part("hmask").unsqueeze(2).to_broadcast([P, H, CTX]), ALU.mult).then_inc(kb_ready, 1)

            pool.wait_ge(consts_set, 5)
            pool.wait_ge(pa_in, 16)
            step_(Step(-2))
            pool.wait_ge(w_summed, 5)
            pool.partition_all_reduce(wtot[:, 0:3], wsum[:, 0:3], P, RADD).then_inc(w_totalled, 1)
            pool.partition_all_reduce(wtot[:, 3:5], wsum[:, 3:5], P, RMAX).then_inc(w_totalled, 1)
            step_(Step(-1))
            s.landed(pool, setup1, "keys1")
            for b in range(1, B):
                block_keys(0, b)
                block_keys(1, b)
            step_(Step(0))
            middle_and_end(pool, step_)

        @block.scalar
        def _(act):
            def keys_values(layer, setup, bias):
                keys = s.see(act, setup, f"keys{layer}")
                act.activation(KT[layer][:, :], keys[:, 0:B * CTX], ACT.Identity, bias=bias).then_inc(s.out, 1)
                values = t.see(act, setup, f"v{layer}")
                act.wait_ge(consts_set, 3)
                act.activation(heads(V[layer][:, :], VW)[:, :, 0:DH], heads(values[0:CTX, :], DH), ACT.Copy)\
                   .then_inc(t.out, 1)

            def step_(step):
                c = step.c
                a, f, p = c + 2, c + 1, c - 1

                def out(where, name, dst, fn=ACT.Copy, width=P, **kw):
                    product = where.see(act, step, name)
                    act.activation(dst, product[0:dst.shape[0], 0:width], fn, **kw).then_inc(where.out, 1)

                def gelu_pair():
                    for n, (where, name) in enumerate(((g, "g_h0"), (u, "g_h1"))):
                        product = where.see(act, step, name)
                        for i in range(2):
                            k = 2 * n + i
                            ins = act.activation(hT[:, k, :], product[:, i * 2 * P:(i + 1) * 2 * P], ACT.Gelu,
                                                 bias=part("bfc")[:, k:k + 1])
                        ins.then_inc(where.out, 1)

                if step.has("G"):
                    gelu_pair()
                if step.has("A"):
                    out(m, "a_xT", xT["a"][:, :])
                if step.has("F"):
                    act.wait_ge(actA_ready, step.done(f + 1))
                    act.activation(yq[:, :], cen["f"][:, f % 2, :], ACT.Copy, scale=actA[:, f % 2:f % 2 + 1], bias=ROUND)\
                       .then_inc(yq_ready, 1)
                    out(m, "f_yT", yqT[:, :], ACT.Copy, bias=-ROUND)
                if step.has("A"):
                    out(m, "a_q", qT["a"][:, :], ACT.Identity, bias=part("bq0"))
                    if a >= 1:
                        act.wait_ge(s0_shifted, step.done(a))
                        act.sem_inc(gate, 1)
                    for i in range(NCH):
                        out(s, f"a_s{i}", s0[:, i * SC:(i + 1) * SC], width=SC, scale=ISQ)
                if step.has("G"):
                    gg = (c - 3) // 2
                    if gg >= 1:
                        act.wait_ge(y_stored, step.pairs(gg, 16))
                        act.sem_inc(gate, 1)
                    product = u.see(act, step, "g_out")
                    act.activation(y[:, :, :], product[:, 0:2 * D].rearrange("p (i d) -> p i d", i=2), ACT.Copy)\
                       .then_inc(u.out, 1)
                if step.has("F"):
                    if f >= 1:
                        act.wait_ge(hid_ready, step.done(f))
                        act.sem_inc(gate, 1)
                    out(g, "f_g", relu_g[:, :], ACT.Relu, width=FF)
                    out(u, "f_u", up_s[:, :], width=FF)
                if step.has("C"):
                    act.wait_ge(sm1_ready, step.done(p + 1))
                    if p >= 1:
                        act.wait_ge(p1_ready, step.done(p))
                    act.activation(e1[:, :], sm1[:, :], ACT.Exp).then_inc(e1_ready, 1)
                    act.activation(mask[:, :], rest[p % 2][:, :], ACT.Relu, bias=-0.5, scale=1.0 / TAKEN)\
                       .then_inc(mask_ready, 1)
                if step.has("F"):
                    act.wait_ge(hA_ready, step.done(f + 1))
                    act.activation(hq[:, :], hid[:, :], ACT.Copy, scale=hA[:, f % 2:f % 2 + 1], bias=ROUND)\
                       .then_inc(hq_ready, 1)
                if step.has("A"):
                    act.wait_ge(s0_shifted, step.done(a + 1))
                    act.activation(e0[:, :], e0[:, :], ACT.Exp).then_inc(e0_ready, 1)
                if step.has("F"):
                    out(g, "f_hT", hqT[:, :], ACT.Copy, width=FF, bias=-ROUND)
                for k, tile in (("a", a), ("c", p)):
                    if not step.has(k.upper()):
                        continue
                    for i in range(NCH):
                        out(t, f"{k}_t{i}", pT[k][:, i * HC * P:(i + 1) * HC * P], width=HC * P)
                    if tile >= 1:
                        act.wait_ge(on_ready[k], step.done(tile))
                        act.sem_inc(gate, 1)
                    out(o, f"{k}_o", osb[k][:, :], width=H * VW)
                if step.has("F"):
                    out(m, "f_xT", xT["d"][:, :])
                    out(m, "f_q", qT["d"][:, :], ACT.Identity, bias=part("bq1"))
                    if f >= 2:
                        act.wait_ge(sm1_ready, step.done(f - 1))
                        act.sem_inc(gate, 1)
                    for i in range(NCH):
                        out(s, f"f_s{i}", s1[f % 2][:, i * SC:(i + 1) * SC], width=SC, scale=ISQ)
                if step.has("A"):
                    out(m, "a_oT", oT["a"][:, :])
                    if a >= 2:
                        u.landed(act, step, "f_down", back=1)
                        act.sem_inc(gate, 1)
                    out(m, "a_out", x1[:, a % 2, :])
                if step.has("C"):
                    out(m, "c_oT", oT["c"][:, :])
                    out(m, "c_out", x3[:, p % 2, :])
                    out(m, "c_xT", x4T[:, p % 2, :])

            keys_values(0, setup0, part("bk0"))
            step_(Step(-2))
            keys_values(1, setup1, part("bk1"))
            step_(Step(-1))
            step_(Step(0))
            middle_and_end(act, step_)

        @block.tensor
        def _(pe):
            def keys_values(layer, setup):
                keys = s.take(pe, setup, f"keys{layer}")
                pe.matmul(keys[:, 0:B * CTX], part(f"wk{layer}"), part("ctx"), start=True, stop=True)\
                  .then_inc(s.full, 1)
                values = t.take(pe, setup, f"v{layer}")
                for b in range(B):
                    dst = values[0:CTX, b * D:(b + 1) * D]
                    pe.matmul(dst, part("ctx")[:, b * CTX:(b + 1) * CTX], part(f"wv{layer}"), start=True, stop=False)
                    ins = pe.matmul(dst, ones[0:1, 0:CTX], part(f"bv{layer}"), start=False, stop=True)
                ins.then_inc(t.full, 1)

            def transpose(step, name, src):
                dst = m.take(pe, step, name)
                pe.transpose(dst[:, 0:P], src, ident).then_inc(m.full, 1)

            def project(step, name, k, w):
                dst = m.take(pe, step, name)
                m.landed(pe, step, f"{name[0]}_xT")
                pe.matmul(dst[:, 0:P], part(w), xT[k][:, :], start=True, stop=True).then_inc(m.full, 1)

            def scores(step, name, k, layer, tile):
                m.landed(pe, step, f"{name}_q")
                b = step.batch(tile)
                for i in range(NCH):
                    dst = s.take(pe, step, f"{name}_s{i}")
                    keys = KB[layer][:, bass.ds(b * HJ + i * SC, SC)]
                    pe.matmul(dst[:, 0:SC], qT[k][:, :], keys, start=True, stop=True).then_inc(s.full, 1)

            def weigh(step, k, layer, tile, src, ready):
                pe.wait_ge(ready, step.done(tile + 1))
                b = step.batch(tile)

                def turn(i):
                    dst = t.take(pe, step, f"{k}_t{i}")
                    for n in range(HC):
                        h = i * HC + n
                        ins = pe.transpose(dst[0:CTX, n * P:(n + 1) * P], src[:, h * CTX:(h + 1) * CTX], ident)
                    ins.then_inc(t.full, 1)

                turn(0)
                turn(1)
                dst = o.take(pe, step, f"{k}_o")
                for i in range(NCH):
                    t.landed(pe, step, f"{k}_t{i}")
                    for n in range(HC):
                        h = i * HC + n
                        ins = pe.matmul(dst[:, h * VW:(h + 1) * VW], pT[k][:, h * P:(h + 1) * P],
                                        V[layer][:, bass.ds(b * H * VW + h * VW, VW)], start=True, stop=True)
                    if i + 2 < NCH:
                        turn(i + 2)
                ins.then_inc(o.full, 1)

            def residual(step, name, k, w, bias, x):
                dst = m.take(pe, step, name)[:, 0:D]
                m.landed(pe, step, f"{k}_oT")
                pe.matmul(dst, oT[k][:, :], part(w), start=True, stop=False)
                pe.matmul(dst, ones[:, :], part(bias), start=False, stop=False)
                pe.matmul(dst, ident, x, start=False, stop=True).then_inc(m.full, 1)

            def step_(step):
                c = step.c
                a, f, p = c + 2, c + 1, c - 1
                if step.has("G"):
                    m.landed(pe, step, "c_xT", back=1)
                    for n, (where, name) in enumerate(((g, "g_h0"), (u, "g_h1"))):
                        dst = where.take(pe, step, name)
                        for i in range(2):
                            k = 2 * n + i
                            ins = pe.matmul(dst[:, i * 2 * P:(i + 1) * 2 * P], fcW[:, k * P:(k + 1) * P],
                                            x4T[:, :, :].rearrange("p i t -> p (i t)"), start=True, stop=True)
                        ins.then_inc(where.full, 1)
                if step.has("A"):
                    pe.wait_ge(ln["a"]["normed"], step.done(a + 1))
                    transpose(step, "a_xT", xn["a"][:, :])
                if step.has("F"):
                    pe.wait_ge(yq_ready, step.done(f + 1))
                    transpose(step, "f_yT", yq[:, :])
                if step.has("A"):
                    project(step, "a_q", "a", "wq0")
                    if a == 0:
                        pe.wait_ge(kb_ready, 1)
                    scores(step, "a", "a", 0, a)
                if step.has("G"):
                    g.landed(pe, step, "g_h0")
                    dst = u.take(pe, step, "g_out")
                    for i in range(2):
                        for k in range(FC):
                            pe.matmul(dst[:, i * D:(i + 1) * D], hT[:, k, i * P:(i + 1) * P], projW[:, k * D:(k + 1) * D],
                                      start=(k == 0), stop=False)
                        pe.matmul(dst[:, i * D:(i + 1) * D], ones[:, :], part("bproj"), start=False, stop=False)
                        ins = pe.matmul(dst[:, i * D:(i + 1) * D], ident, x3[:, i, :], start=False, stop=True)
                    ins.then_inc(u.full, 1)
                if step.has("F"):
                    m.landed(pe, step, "f_yT")
                    for where, name, w in ((g, "f_g", gateQ), (u, "f_u", upQ)):
                        dst = where.take(pe, step, name)
                        pe.matmul(dst[:, :], yqT[:, :], w[:, :], start=True, stop=True).then_inc(where.full, 1)
                    pe.wait_ge(hq_ready, step.done(f + 1))
                    dst = g.take(pe, step, "f_hT")
                    for k in range(FC):
                        ins = pe.transpose(dst[:, k * P:(k + 1) * P], hq[:, k * P:(k + 1) * P], ident)
                    ins.then_inc(g.full, 1)
                    dst = u.take(pe, step, "f_down")
                    g.landed(pe, step, "f_hT")
                    for k in range(FC):
                        ins = pe.matmul(dst[:, 0:D], hqT[:, k * P:(k + 1) * P], downQ[:, k * D:(k + 1) * D],
                                        start=(k == 0), stop=(k == FC - 1))
                    ins.then_inc(u.full, 1)
                if step.has("A"):
                    weigh(step, "a", 0, a, e0, e0_ready)
                if step.has("C"):
                    weigh(step, "c", 1, p, p1, p1_ready)
                if step.has("F"):
                    pe.wait_ge(ln["d"]["normed"], step.done(f + 1))
                    transpose(step, "f_xT", xn["d"][:, :])
                    project(step, "f_q", "d", "wq1")
                    if f == 0:
                        pe.wait_ge(kb_ready, 2)
                    scores(step, "f", "d", 1, f)
                if step.has("A"):
                    pe.wait_ge(on_ready["a"], step.done(a + 1))
                    transpose(step, "a_oT", on["a"][:, :])
                    residual(step, "a_out", "a", "wo0", "bo0", xin[:, a % 2, :])
                if step.has("C"):
                    pe.wait_ge(on_ready["c"], step.done(p + 1))
                    transpose(step, "c_oT", on["c"][:, :])
                    pe.wait_ge(x2_kept[p % 2], step.loaded(p))
                    residual(step, "c_out", "c", "wo1", "bo1", x2keep[:, p % 2, :])
                    pe.wait_ge(ln["c"]["normed"], step.done(p + 1))
                    transpose(step, "c_xT", xn["c"][:, :])

            pe.wait_ge(pa_in, 16)
            pe.wait_ge(row_in, 16)
            pe.wait_ge(consts_set, 1)
            keys_values(0, setup0)
            step_(Step(-2))
            pe.wait_ge(pc_in, 16)
            keys_values(1, setup1)
            pe.wait_ge(r16_in, 16)
            pe.matmul(g.take(pe, setup1, "lora_fc")[:, :], part("afc"), part("bfcT"), start=True, stop=True)\
              .then_inc(g.full, 1)
            dst = u.take(pe, setup1, "lora_proj")
            for k in range(FC):
                ins = pe.matmul(dst[:, k * D:(k + 1) * D], part("aproj")[:, k * P:(k + 1) * P], part("bprojT"),
                                start=True, stop=True)
            ins.then_inc(u.full, 1)
            pe.wait_ge(w_ready, 3)
            step_(Step(-1))
            pe.wait_ge(kb_ready, 2 * B)
            step_(Step(0))
            middle_and_end(pe, step_)

        @block.sync
        def _(sp):
            x_t = x.rearrange("(t p) d -> t p d", p=P)
            out_g = out.rearrange("(g i p) d -> g p i d", i=2, p=P)

            def step_(step):
                c = step.c
                a, f = c + 2, c + 1
                if step.has("A"):
                    if a >= 2:
                        n, per_pair = m.turn(step, "a_out", back=2)
                        sp.wait_ge(m.full, step.plus(n + 1, per_pair))
                    sp.dma_start(xin[:, a % 2, :], x_t[step.plus(a, 2)]).then_inc(x_in[a % 2], 16)
                if c >= 0 and has("F", c - 1):
                    u.landed(sp, step, "f_down", back=1)
                    sp.sem_inc(gate, 1)
                    ln_d = step.done(c + 1)
                    sp.wait_ge(ln["d"]["normed"], ln_d)
                    if c >= 2:
                        sp.sem_inc(gate, 1)
                        m.used(sp, step, "c_out", back=1)
                    sp.dma_start(x2keep[:, c % 2, :], x2[:, c % 2, :]).then_inc(x2_kept[c % 2], 16)
                if c >= FIRST + 1:
                    sp.wait_ge(dve_over, step.plus(c - FIRST, 2))
                    sp.sem_inc(gate, 1)
                    sp.wait_ge(dve_step[(c - 1) % 2], dve_counts[standing_for(c - 1)])
                    sp.sem_inc(gate, 1)
                    sp.sem_clear(dve_step[(c - 1) % 2])
                    sp.sem_inc(dve_cleared, 1)
                if step.has("G"):
                    gg = (c - 3) // 2
                    u.landed(sp, step, "g_out")
                    sp.dma_start(out_g[step.pairs(gg, 1)], y[:, :, :]).then_inc(y_stored, 16)

            sp.dma_start(pa_s[:, :], pa).then_inc(pa_in, 16)
            sp.dma_start(row_s[:, :], rows).then_inc(row_in, 16)
            step_(Step(-2))
            sp.dma_start(pb_s[:, :], pb).then_inc(pb_in, 16)
            sp.dma_start(pc_s[:, :], pc).then_inc(pc_in, 16)
            sp.dma_start(r16_s[:, :], r16).then_inc(r16_in, 16)
            step_(Step(-1))
            step_(Step(0))
            middle_and_end(sp, step_)
            sp.wait_ge(y_stored, 16 * (TILES // 2))


DUE = {"a_stats": 0, "f_stats": 1, "f_scale": 12, "a_max": 36, "f_hidden": 54, "f_residual": 70, "a_recip": 92,
       "c_recip": 106, "c_stats": 124}


def kernel(x, ctx_1024, **w):
    import numpy as np
    import concourse.bacc as bacc
    from concourse.bass_utils import run_bass_kernel_spmd

    w = {k: np.asarray(v) for k, v in w.items()}
    x, ctx_1024 = np.asarray(x), np.asarray(ctx_1024)

    def col(v):
        return v.reshape(-1, P).T

    def chunked(v):
        return v.T.reshape(FC, P, D).transpose(1, 0, 2).reshape(P, FF)

    dt = x.dtype
    ident = np.eye(P, dtype=dt)
    hmask = np.repeat(np.eye(H, dtype=dt), DH, axis=0)
    ctxT = ctx_1024.reshape(B * CTX, D).T
    pa = np.concatenate([ident, hmask, col(w["L0_xattn_b_q"]), col(w["L0_xattn_b_k"]), w["L0_xattn_w_q"].T,
                         w["L0_xattn_w_k"].T, w["L0_xattn_w_v"].T, w["L0_xattn_w_o"].T, ctxT], axis=1)
    pb = np.concatenate([w["L0_ffn_w_gate"].T, w["L0_ffn_w_up"].T, chunked(w["L0_ffn_w_down"])], axis=1)
    pc = np.concatenate([w["L1_xattn_Wq"].T, w["L1_xattn_Wk"].T, w["L1_xattn_Wv"].T, w["L1_xattn_Wo"].T,
                         col(w["L1_xattn_bq"]), col(w["L1_xattn_bk"]), col(w["L1_ffn_b_fc"]), w["L1_ffn_W_fc"].T,
                         chunked(w["L1_ffn_W_proj"])], axis=1)
    rows = np.concatenate([w["L0_xattn_b_v"], w["L0_xattn_b_o"], w["L1_xattn_bv"], w["L1_xattn_bo"],
                           w["L1_ffn_b_proj"]])[None, :]
    r16 = np.concatenate([w["L1_ffn_A_fc"], w["L1_ffn_B_fc"].T, w["L1_ffn_A_proj"], w["L1_ffn_B_proj"].T], axis=1)
    arrays = {"x": x.reshape(B * S, D), "pa": pa, "pb": pb, "pc": pc, "rows": rows, "r16": r16}
    arrays = {f"in_{k}": np.ascontiguousarray(v) for k, v in arrays.items()}

    nc = bacc.Bacc("TRN2", target_bir_lowering=False, num_devices=1)
    args = [nc.dram_tensor(k, v.shape, mybir.dt.from_np(v.dtype), kind="ExternalInput").ap() for k, v in arrays.items()]
    out = nc.dram_tensor("out_y", (B * S, D), F32, kind="ExternalOutput").ap()
    build(nc, *args, out)
    r = run_bass_kernel_spmd(nc, [arrays], core_ids=[0])
    return r.results[0]["out_y"].reshape(B, S, D)
```

```python
from contextlib import ExitStack

import concourse.bass as bass
from concourse import mybir

F32 = mybir.dt.float32
BF16 = mybir.dt.bfloat16
ALU = mybir.AluOpType
ACT = mybir.ActivationFunctionType
X = mybir.AxisListType.X
RMAX = bass.bass_isa.ReduceOp.max
RADD = bass.bass_isa.ReduceOp.add

B, S, D = 4, 512, 128
CTX = 77
H = 16
DH = D // H
FF = 512
FC = FF // D
RANK = 16
P = 128
TILES = B * S // P
TPB = S // P
HC = 4
NCH = H // HC
SC = HC * CTX
HJ = H * CTX
VW = DH + 1
WC = -(-HJ // P)
WH = 3
TURN = 4
NT = -(-WC // TURN)
VB_W = WC * WH * VW + (H - WH) * VW
REP = 3 * CTX
ROW_PARTS = 3
ROUNDS = 4
LN_EPS = 1e-5
Q_EPS = 1e-5
LORA_SCALE = 2.0
ROUND = 12582912.0
TAKEN = -float(2 ** 120)
ISQ = float(DH) ** -0.5

def start(i):
    return min(i * P, HJ - P)


def first_head(i):
    return min(start(i) // CTX, H - WH)


def place(i):
    return (i - 1) % WC


PA = {}
PB = {}
PC = {}
ROW = {}
R16 = {}


def _lay(table, *parts):
    at = 0
    for name, width in parts:
        table[name] = (at, at + width)
        at += width
    return at


PA_W = _lay(PA, ("ident", P), ("hmask", H), ("bq0", 1), ("bk0", 1), ("bv0", 1), ("vmask", WC * WH), ("wq0", D), ("wk0", D), ("wv0", D), ("wo0", D),
            ("ctx", B * CTX))
PB_W = _lay(PB, ("gate", FF), ("up", FF), ("down", FF))
PC_W = _lay(PC, ("wq1", D), ("wk1", D), ("wv1", D), ("wo1", D), ("bq1", 1), ("bk1", 1), ("bv1", 1), ("bfc", FC), ("fc", FF),
            ("proj", FF))
ROW_W = _lay(ROW, ("bo0", D), ("bo1", D), ("bproj", D))
R16_W = _lay(R16, ("afc", D), ("bfcT", FF), ("aproj", FF), ("bprojT", D))

AT = {"L": 4, "A": 3, "E": 2, "F": 2, "D": 1, "Q": 1, "T": 0, "C": -1, "N": -2}
FIRST, LAST = -AT["A"], TILES + 1
LOOP = (4, 5)
LOOPS = (TILES - AT["L"] - LOOP[0]) // 2


def has(stage, c):
    if stage == "G":
        return c % 2 == 1 and 3 <= c <= LAST
    return 0 <= c + AT[stage] < TILES


class Step:

    def __init__(self, c, j=None):
        self.c, self.j = c, j

    def has(self, stage):
        return has(stage, self.c)

    def plus(self, fixed, per_pair):
        return fixed if self.j is None or per_pair == 0 else self.j * per_pair + fixed

    def done(self, tile, per_tile=1, more=0):
        return self.plus(per_tile * tile + more, 2 * per_tile)

    def loaded(self, tile):
        return self.plus(16 * (tile // 2 + 1), 16)

    def pairs(self, g, per_pair=1, more=0):
        return self.plus(per_pair * g + more, per_pair)

    def batch(self, tile):
        if self.j is None:
            return tile // TPB
        return (self.j + tile // 2) // (TPB // 2)


def standing_for(c):
    return LOOP[c % 2] if LOOP[0] <= c < LOOP[0] + 2 * LOOPS else c


ORDER = ["setup0", FIRST, "setup1"] + list(range(FIRST + 1, LAST + 1))


class Bank:

    def __init__(self, tensors, full, out, setup0, setup1, names):
        self.tensors, self.full, self.out = tensors, full, out
        self.fixed = {"setup0": setup0, "setup1": setup1}
        self.names = names

    def users(self, key):
        if key in self.fixed:
            return self.fixed[key]
        return [n for n in self.names if has(n[0].upper(), key)]

    def turn(self, step, name, back=0):
        key = step.c if not back else step.c - back
        if step.j is not None:
            assert self.users(key) == self.users(key + 2)
        before = sum(len(self.users(k)) for k in ORDER[:ORDER.index(key)])
        return before + self.users(key).index(name), sum(len(self.users(k)) for k in LOOP)

    def slot(self, step, name):
        n, per_pair = self.turn(step, name)
        assert step.j is None or per_pair % len(self.tensors) == 0
        return self.tensors[n % len(self.tensors)]

    def take(self, pe, step, name):
        n, per_pair = self.turn(step, name)
        n -= len(self.tensors) - 1
        if n > 0:
            pe.wait_ge(self.out, step.plus(n, per_pair))
        return self.slot(step, name)

    def see(self, eng, step, name):
        n, per_pair = self.turn(step, name)
        eng.wait_ge(self.full, step.plus(n + 1, per_pair))
        return self.slot(step, name)

    def landed(self, eng, step, name, back=0):
        n, per_pair = self.turn(step, name, back)
        eng.wait_ge(self.out, step.plus(n + 1, per_pair))

    def used(self, eng, step, name, back=0):
        n, per_pair = self.turn(step, name, back)
        eng.wait_ge(self.full, step.plus(n + 1, per_pair))


def build(nc, x, pa, pb, pc, rows, r16, out):
    with ExitStack() as ctx:
        def sb(name, shape, dt=F32):
            return ctx.enter_context(nc.sbuf_tensor(name, shape, dt))

        def sem(name):
            return ctx.enter_context(nc.semaphore(name))

        pa_s, pb_s, pc_s = sb("pa_s", [P, PA_W]), sb("pb_s", [P, PB_W]), sb("pc_s", [P, PC_W])
        row_s, r16_s = sb("row_s", [ROW_PARTS, ROW_W]), sb("r16_s", [RANK, R16_W])

        def part(name):
            for tensor, table in ((pa_s, PA), (pb_s, PB), (pc_s, PC), (r16_s, R16)):
                if name in table:
                    return tensor[:, table[name][0]:table[name][1]]

        def row(name):
            return row_bf[:, 1, ROW[name][0]:ROW[name][1]]

        ident = part("ident")
        ones = sb("ones", [ROW_PARTS, P], BF16)
        row_part = sb("row_part", [ROW_PARTS, ROW_PARTS, ROW_W], BF16)
        row_rest = sb("row_rest", [ROW_PARTS, 2, ROW_W])
        row_own = sb("row_own", [ROW_PARTS, ROW_PARTS, ROW_W], BF16)
        row_zero = sb("row_zero", [ROW_PARTS, ROW_W])
        row_bf = sb("row_bf", [ROW_PARTS, 2, ROW_W], BF16)
        eps, mhalf = sb("eps", [P, 1]), sb("mhalf", [P, 1])
        wsum = sb("wsum", [P, 8])
        wtot = sb("wtot", [P, 8])
        wscale = sb("wscale", [P, 8])
        wrec = sb("wrec", [P, 8])
        wcub = sb("wcub", [P, 2])
        wtmp = sb("wtmp", [P, 2, FF])
        gateQ, upQ, downQ = (sb(n, [P, FF], BF16) for n in ("gateQ", "upQ", "downQ"))
        fcW, projW = sb("fcW", [P, FF]), sb("projW", [P, FF])
        KT = [sb(f"KT{l}", [P, B * CTX]) for l in range(2)]
        KB = [sb(f"KB{l}", [P, B * HJ]) for l in range(2)]
        ctx3 = sb("ctx3", [P, B * REP])
        V = [sb(f"V{l}", [P, B * VB_W]) for l in range(2)]

        xin = sb("xin", [P, 2, D])
        stats = {k: sb(f"stats_{k}", [P, 2, 6]) for k in "afqn"}
        mv = {k: sb(f"mv_{k}", [P, 2, 2]) for k in "afqn"}
        ve = {k: sb(f"ve_{k}", [P, 1]) for k in "afqn"}
        rstd = {k: sb(f"rstd_{k}", [P, 2]) for k in "afqn"}
        cen = {k: sb(f"cen_{k}", [P, 2, D]) for k in "afqn"}
        xn = {k: sb(f"xn_{k}", [P, D]) for k in "aqn"}
        xT = {k: sb(f"xT_{k}", [P, P]) for k in "aq"}
        qT = {k: sb(f"qT_{k}", [P, P]) for k in "aq"}
        s0, e0 = sb("s0", [P, HJ]), sb("e0", [P, HJ])
        nmax = sb("nmax", [P, 2, H])
        pT = {k: sb(f"pT_{k}", [P, WC * P]) for k in "ec"}
        osb = {k: sb(f"osb_{k}", [P, H * VW]) for k in "ec"}
        rden = {k: sb(f"rden_{k}", [P, 2, H]) for k in "ec"}
        on = {k: sb(f"on_{k}", [P, D]) for k in "ec"}
        oT = {k: sb(f"oT_{k}", [P, P]) for k in "ec"}
        x1, x2, x2keep, x3 = (sb(n, [P, 2, D]) for n in ("x1", "x2", "x2keep", "x3"))
        amax = sb("amax", [P, 2, 4])
        actA = sb("actA", [P, 2])
        yq, yqT = sb("yq", [P, P]), sb("yqT", [P, P], BF16)
        cub = sb("cub", [P, 3])
        relu_g, up_s, prod, hid = (sb(n, [P, FF]) for n in ("relu_g", "up_s", "prod", "hid"))
        hmax = sb("hmax", [P, 2, 4])
        hA, osc = sb("hA", [P, 2]), sb("osc", [P, 2])
        hq, hqT = sb("hq", [P, FF]), sb("hqT", [P, FF], BF16)
        s1 = [sb(f"s1_{i}", [P, HJ]) for i in range(2)]
        rest = [sb(f"rest_{i}", [P, HJ]) for i in range(2)]
        top = sb("top", [P, 2, H, ROUNDS, 8])
        sm1, e1, mask, p1 = (sb(n, [P, HJ]) for n in ("sm1", "e1", "mask", "p1"))
        x4T = sb("x4T", [P, 2, P])
        hT = sb("hT", [P, FC, 2 * P])
        y = sb("y", [P, 2, D])
        mark = sb("mark", [1, 2])

        pa_in, pb_in, pc_in, row_in, r16_in = (sem(n) for n in ("pa_in", "pb_in", "pc_in", "row_in", "r16_in"))
        consts_set, kb_ready, ctx3_ready = sem("consts_set"), sem("kb_ready"), sem("ctx3_ready")
        row_split = sem("row_split")
        w_summed, w_totalled, w_chain, w_ready = (sem(n) for n in ("w_summed", "w_totalled", "w_chain", "w_ready"))
        x_in, x2_kept = [sem("x_in_even"), sem("x_in_odd")], [sem("x2_kept_even"), sem("x2_kept_odd")]
        y_stored = sem("y_stored")
        gate = sem("gate")
        dve_step = [sem("dve_step_even"), sem("dve_step_odd")]
        dve_over, dve_cleared = sem("dve_over"), sem("dve_cleared")
        ln = {k: {n: sem(f"{k}_{n}") for n in ("stats", "chain", "centred", "normed")} for k in "afqn"}
        nmax_ready, s0_shifted, e0_ready = sem("nmax_ready"), sem("s0_shifted"), sem("e0_ready")
        rden_ready = {k: sem(f"rden_ready_{k}") for k in "ec"}
        on_ready = {k: sem(f"on_ready_{k}") for k in "ec"}
        actA_ready, yq_ready, cub_chain, cub_ready = (sem(n) for n in ("actA_ready", "yq_ready", "cub_chain", "cub_ready"))
        prod_ready, hid_ready, hA_ready, hq_ready = (sem(n) for n in ("prod_ready", "hid_ready", "hA_ready", "hq_ready"))
        top_ready, sm1_ready, e1_ready, mask_ready, p1_ready = (
            sem(n) for n in ("top_ready", "sm1_ready", "e1_ready", "mask_ready", "p1_ready"))

        banks = [ctx.enter_context(nc.psum_tensor(f"bank{i}", [P, 512], F32)) for i in range(8)]

        def bank(name, tensors, setup0, setup1, names):
            return Bank(tensors, sem(f"{name}_full"), sem(f"{name}_out"), setup0, setup1, names)

        m = bank("m", [banks[0]], [], [],
                 ["a_xT", "a_q", "n_xT", "e_oT", "e_out", "q_xT", "q_q", "f_yT", "c_oT", "c_out"])
        o = bank("o", [banks[1]], [], [], ["e_o", "c_o"])
        g = bank("g", [banks[2]], [], ["lora_fc"], ["d_hT", "g_h0", "f_g"])
        u = bank("u", [banks[3]], [], ["lora_proj"], ["d_down", "g_h1", "f_u", "g_out"])
        s = bank("s", banks[4:6], ["keys0"], ["keys1"], [f"{k}_s{i}" for k in "aq" for i in range(NCH)])
        t = bank("t", banks[6:8], ["v0_0", "v0_1"], ["v1_0", "v1_1"],
                 [f"{k}_t{i}" for k in "ec" for i in range(NT)])
        setup0, setup1 = Step("setup0"), Step("setup1")

        def heads(ap, w=CTX):
            return ap.rearrange("p (h j) -> p h j", j=w)

        def values_of(layer):
            return V[layer][:, :].rearrange("p (b w) -> p b w", b=B)[:, :, 0:WC * WH * VW]\
                .rearrange("p b (k v) -> p b k v", v=VW)

        def middle_and_end(eng, step_):
            for c in range(FIRST + 1, LOOP[0]):
                step_(Step(c))
            with eng.Fori(0, LOOPS) as j:
                for c in LOOP:
                    step_(Step(c, j))
            for c in range(LOOP[0] + 2 * LOOPS, LAST + 1):
                step_(Step(c))

        block = ctx.enter_context(nc.Block())
        dve_counts = {}

        @block.vector
        def _(dve):
            dve.memset(ones[:, :], 1.0).then_inc(consts_set, 1)
            for l in range(2):
                dve.memset(V[l].rearrange("p (b w) -> p b w", b=B)[:, :, WC * WH * VW:], 0.0).then_inc(consts_set, 1)
            dve.memset(eps[:, :], LN_EPS).then_inc(consts_set, 1)
            dve.memset(mhalf[:, :], -0.5).then_inc(consts_set, 1)
            dve.memset(row_zero[:, :], 0.0).then_inc(consts_set, 1)

            class Own:

                def __init__(self, step):
                    self.sem, self.n = dve_step[step.c % 2], 0

                def out(self, ins):
                    self.n += 1
                    ins.then_inc(self.sem, 1)
                    return self.n

                def wait(self, n):
                    dve.wait_ge(self.sem, n)

            def ln_stats(own, step, k, src, tile):
                par = tile % 2
                if tile >= 2:
                    dve.wait_ge(ln[k]["normed"], step.done(tile - 1))
                n = own.out(dve.bn_stats(stats[k][:, par, :], src))
                own.wait(n)
                dve.bn_aggr(mv[k][:, par, :], stats[k][:, par, :]).then_inc(ln[k]["stats"], 1)

            def a_stats(own, step):
                a = step.c + AT["A"]
                dve.wait_ge(x_in[a % 2], step.loaded(a))
                ln_stats(own, step, "a", xin[:, a % 2, :], a)

            def a_max(own, step):
                a = step.c + AT["A"]
                s.landed(dve, step, f"a_s{NCH - 1}")
                dve.tensor_reduce(nmax[:, a % 2, :], heads(s0[:, :]), X, ALU.max, negate=True).then_inc(nmax_ready, 1)

            def recip(step, k):
                tile = step.c + AT[k.upper()]
                o.landed(dve, step, f"{k}_o")
                dve.reciprocal(rden[k][:, tile % 2, :], heads(osb[k][:, :], VW)[:, :, DH]).then_inc(rden_ready[k], 1)

            def f_stats(own, step):
                f = step.c + AT["F"]
                m.landed(dve, step, "e_out")
                ln_stats(own, step, "f", x1[:, f % 2, :], f)

            def f_scale(own, step):
                f = step.c + AT["F"]
                par = f % 2
                a_ = amax[:, par, :]
                dve.wait_ge(ln["f"]["centred"], step.done(f + 1))
                n = own.out(dve.tensor_reduce(a_[:, 0:1], cen["f"][:, par, :], X, ALU.max, apply_absolute_value=True))
                dve.wait_ge(ln["f"]["normed"], step.done(f + 1))
                own.wait(n)
                n = own.out(dve.tensor_tensor(a_[:, 1:2], a_[:, 0:1], rstd["f"][:, par:par + 1], ALU.mult))
                own.wait(n)
                n = own.out(dve.tensor_scalar(a_[:, 2:3], a_[:, 1:2], Q_EPS, 1.0 / 127.0, ALU.max, ALU.mult))
                own.wait(n)
                n = own.out(dve.reciprocal(a_[:, 3:4], a_[:, 2:3]))
                own.wait(n)
                dve.tensor_tensor(actA[:, par:par + 1], a_[:, 3:4], rstd["f"][:, par:par + 1], ALU.mult)\
                   .then_inc(actA_ready, 1)

            def d_hidden_scale(own, step):
                d = step.c + AT["D"]
                par = d % 2
                h_ = hmax[:, par, :]
                dve.wait_ge(hid_ready, step.done(d + 1))
                n = own.out(dve.tensor_reduce(h_[:, 0:1], hid[:, :], X, ALU.max, apply_absolute_value=True))
                dve.wait_ge(cub_ready, step.done(d + 1))
                own.wait(n)
                n = own.out(dve.tensor_tensor(h_[:, 1:2], h_[:, 0:1], cub[:, 2:3], ALU.mult))
                own.wait(n)
                n = own.out(dve.tensor_scalar(h_[:, 2:3], h_[:, 1:2], Q_EPS, 1.0 / 127.0, ALU.max, ALU.mult))
                own.wait(n)
                n = own.out(dve.reciprocal(h_[:, 3:4], h_[:, 2:3]))
                osc_made = own.out(dve.tensor_tensor(osc[:, par:par + 1], h_[:, 2:3], wscale[:, 2:3], ALU.mult))
                own.wait(n)
                dve.tensor_tensor(hA[:, par:par + 1], h_[:, 3:4], cub[:, 2:3], ALU.mult).then_inc(hA_ready, 1)
                return osc_made

            def d_residual(own, step, osc_made):
                d = step.c + AT["D"]
                par = d % 2
                product = u.see(dve, step, "d_down")
                if d >= 2:
                    dve.wait_ge(x2_kept[par], step.loaded(d - 2))
                    dve.wait_ge(ln["q"]["centred"], step.done(d - 1))
                own.wait(osc_made)
                dve.scalar_tensor_tensor(x2[:, par, :], product[:, 0:D], osc[:, par:par + 1], x1[:, par, :],
                                         ALU.mult, ALU.add).then_inc(u.out, 1)
                u.landed(dve, step, "d_down")
                ln_stats(own, step, "q", x2[:, par, :], d)

            def n_stats(own, step):
                n = step.c + AT["N"]
                m.landed(dve, step, "c_out", back=1)
                ln_stats(own, step, "n", x3[:, n % 2, :], n)

            def top_rounds(own, step):
                par = step.c % 2
                scores, marked = heads(s1[par][:, :]), heads(rest[par][:, :])
                for h0 in range(0, H, 8):
                    made = {}
                    for r in range(ROUNDS):
                        src = marked if r else scores
                        for h in range(h0, h0 + 8):
                            if r:
                                own.wait(made[h])
                            made[h] = own.out(dve.max(top[:, par, h, r, :], src[:, h, :]))
                            yield
                        for h in range(h0, h0 + 8):
                            own.wait(made[h])
                            ins = dve.match_replace(marked[:, h, :], top[:, par, h, r, :], src[:, h, :], TAKEN)
                            if r == ROUNDS - 1:
                                ins.then_inc(top_ready, 1)
                            else:
                                made[h] = own.out(ins)
                            yield

            def step_(step):
                c = step.c
                own = Own(step)
                if c >= FIRST + 2:
                    dve.wait_ge(dve_cleared, step.plus(c - FIRST - 1, 2))
                    dve.sem_inc(gate, 1)
                if step.has("T"):
                    s.landed(dve, step, f"q_s{NCH - 1}", back=1)
                    dve.sem_inc(gate, 1)
                    if c >= 2:
                        dve.wait_ge(mask_ready, step.done(c - 1))
                        dve.sem_inc(gate, 1)
                        dve.wait_ge(sm1_ready, step.done(c - 1))
                        dve.sem_inc(gate, 1)
                small, kept = [], {}
                parts = {
                    "A": {"a_stats": lambda: a_stats(own, step), "a_max": lambda: a_max(own, step)},
                    "E": {"e_recip": lambda: recip(step, "e")},
                    "F": {"f_stats": lambda: f_stats(own, step), "f_scale": lambda: f_scale(own, step)},
                    "D": {"d_hidden": lambda: kept.update(osc=d_hidden_scale(own, step)),
                          "d_residual": lambda: d_residual(own, step, kept["osc"])},
                    "C": {"c_recip": lambda: recip(step, "c")},
                    "N": {"n_stats": lambda: n_stats(own, step)},
                }
                for stage, group in parts.items():
                    if step.has(stage):
                        small += [(DUE[name], part_) for name, part_ in group.items()]
                small.sort(key=lambda due: due[0])
                if step.has("T"):
                    for n, _ in enumerate(top_rounds(own, step)):
                        while small and small[0][0] <= n:
                            small.pop(0)[1]()
                while small:
                    small.pop(0)[1]()
                dve.memset(mark[:, c % 2:c % 2 + 1], 0.0).then_inc(dve_over, 1)
                dve_counts[c] = own.n

            def block_keys(layer, b):
                dve.tensor_tensor(heads(KB[layer][:, b * HJ:(b + 1) * HJ]),
                                  KT[layer][:, b * CTX:(b + 1) * CTX].unsqueeze(1).to_broadcast([P, H, CTX]),
                                  part("hmask").unsqueeze(2).to_broadcast([P, H, CTX]), ALU.mult).then_inc(kb_ready, 1)

            def mask_values(layer, setup):
                for half in range(2):
                    product = t.see(dve, setup, f"v{layer}_{half}")
                    dve.tensor_tensor(
                        values_of(layer)[:, 2 * half:2 * half + 2, :, 0:DH],
                        product[:, 0:2 * WC * WH * DH].rearrange("p (b k d) -> p b k d", b=2, d=DH),
                        part("vmask").unsqueeze(1).unsqueeze(3).to_broadcast([P, 2, WC * WH, DH]), ALU.mult)\
                       .then_inc(t.out, 1)

            def weight_scales():
                dve.wait_ge(pb_in, 16)
                for i, name in enumerate(("gate", "up", "down")):
                    dve.tensor_reduce(wsum[:, i:i + 1], part(name), X, ALU.add, apply_absolute_value=True)\
                       .then_inc(w_summed, 1)
                dve.wait_ge(pc_in, 16)
                for i, name in enumerate(("fc", "proj")):
                    dve.tensor_reduce(wsum[:, 3 + i:4 + i], part(name), X, ALU.max, apply_absolute_value=True)\
                       .then_inc(w_summed, 1)
                dve.wait_ge(w_totalled, 2)
                dve.tensor_scalar(wscale[:, 0:3], wtot[:, 0:3], 1.0 / (FF * D), Q_EPS, ALU.mult, ALU.max)\
                   .then_inc(w_chain, 1)
                dve.tensor_scalar(wscale[:, 3:5], wtot[:, 3:5], 1.0 / 127.0, None, ALU.mult).then_inc(w_chain, 1)
                dve.wait_ge(w_chain, 2)
                dve.reciprocal(wrec[:, 0:5], wscale[:, 0:5]).then_inc(w_chain, 1)
                dve.tensor_tensor(wcub[:, 0:1], wscale[:, 0:1], wscale[:, 0:1], ALU.mult).then_inc(w_chain, 1)
                dve.wait_ge(w_chain, 4)
                dve.tensor_tensor(wcub[:, 1:2], wcub[:, 0:1], wscale[:, 1:2], ALU.mult).then_inc(w_chain, 1)
                return 5

            def round_weights(chain):
                for i, (name, dst) in enumerate((("gate", gateQ), ("up", upQ), ("down", downQ))):
                    tmp = wtmp[:, i % 2, :]
                    if i == 2:
                        dve.wait_ge(w_ready, 1)
                    dve.tensor_scalar(tmp, part(name), wrec[:, i:i + 1], 1.0, ALU.mult, ALU.min).then_inc(w_chain, 1)
                    dve.wait_ge(w_chain, chain + 1)
                    dve.tensor_scalar(tmp, tmp, -1.0, ROUND, ALU.max, ALU.add).then_inc(w_chain, 1)
                    dve.wait_ge(w_chain, chain + 2)
                    dve.tensor_scalar(dst[:, :], tmp, -ROUND, None, ALU.add).then_inc(w_ready, 1)
                    chain += 2
                dve.wait_ge(w_ready, 3)
                for i, (name, where, user) in enumerate((("fc", g, "lora_fc"), ("proj", u, "lora_proj"))):
                    tmp = wtmp[:, i, :]
                    dve.tensor_scalar(tmp, part(name), wrec[:, 3 + i:4 + i], 127.0, ALU.mult, ALU.min)\
                       .then_inc(w_chain, 1)
                    dve.wait_ge(w_chain, chain + 1)
                    dve.tensor_scalar(tmp, tmp, -128.0, ROUND, ALU.max, ALU.add).then_inc(w_chain, 1)
                    dve.wait_ge(w_chain, chain + 2)
                    dve.tensor_scalar(tmp, tmp, -ROUND, wscale[:, 3 + i:4 + i], ALU.add, ALU.mult).then_inc(w_chain, 1)
                    chain += 3
                    product = where.see(dve, setup1, user)
                    dve.wait_ge(w_chain, chain)
                    dve.scalar_tensor_tensor((fcW, projW)[i][:, :], product[:, :], LORA_SCALE, tmp, ALU.mult, ALU.add)\
                       .then_inc(where.out, 1)

            dve.wait_ge(pa_in, 16)
            s.landed(dve, setup0, "keys0")
            block_keys(0, 0)
            mask_values(0, setup0)
            step_(Step(FIRST))
            chain = weight_scales()
            s.landed(dve, setup1, "keys1")
            block_keys(1, 0)
            mask_values(1, setup1)
            round_weights(chain)
            middle_and_end(dve, step_)

        @block.gpsimd
        def _(pool):
            def norm(step, k, src, tile, turn=None, back=1):
                par = tile % 2
                pool.wait_ge(ln[k]["stats"], step.done(tile + 1))
                if k == "f" and tile >= 2:
                    pool.wait_ge(yq_ready, step.done(tile - 1))
                pool.tensor_tensor(cen[k][:, par, :], src, mv[k][:, par, 0:1].to_broadcast([P, D]), ALU.subtract)\
                    .then_inc(ln[k]["centred"], 1)
                pool.tensor_tensor(ve[k][:, :], mv[k][:, par, 1:2], eps[:, :], ALU.add).then_inc(ln[k]["chain"], 1)
                if turn is None:
                    pool.wait_ge(ln[k]["chain"], step.done(tile + 1))
                    pool.tensor_tensor(rstd[k][:, par:par + 1], ve[k][:, :], mhalf[:, :], ALU.pow)\
                        .then_inc(ln[k]["normed"], 1)
                    return
                pool.wait_ge(ln[k]["chain"], step.done(tile, 2, 1))
                pool.tensor_tensor(rstd[k][:, par:par + 1], ve[k][:, :], mhalf[:, :], ALU.pow)\
                    .then_inc(ln[k]["chain"], 1)
                pool.wait_ge(ln[k]["centred"], step.done(tile + 1))
                if tile >= 1:
                    m.used(pool, step, turn, back=back)
                pool.wait_ge(ln[k]["chain"], step.done(tile, 2, 2))
                pool.tensor_tensor(xn[k][:, :], cen[k][:, par, :], rstd[k][:, par:par + 1].to_broadcast([P, D]),
                                   ALU.mult).then_inc(ln[k]["normed"], 1)

            def heads_out(step, k, tile):
                pool.wait_ge(rden_ready[k], step.done(tile + 1))
                if tile >= 1:
                    m.used(pool, step, f"{k}_oT", back=1)
                pool.tensor_tensor(heads(on[k][:, :], DH), heads(osb[k][:, :], VW)[:, :, 0:DH],
                                   rden[k][:, tile % 2, :].unsqueeze(2).to_broadcast([P, H, DH]), ALU.mult)\
                    .then_inc(on_ready[k], 1)

            def step_(step):
                a, e, f, q, p, n = (step.c + AT[k] for k in "AEFQCN")
                if step.has("A"):
                    norm(step, "a", xin[:, a % 2, :], a, "a_xT")
                if step.has("C"):
                    pool.wait_ge(top_ready, step.done(p + 1, H))
                    if p >= 1:
                        pool.wait_ge(e1_ready, step.done(p))
                    pool.tensor_tensor(heads(sm1[:, :]), heads(s1[p % 2][:, :]),
                                       top[:, p % 2, :, 0, 0:1].to_broadcast([P, H, CTX]), ALU.subtract)\
                        .then_inc(sm1_ready, 1)
                if step.has("N"):
                    norm(step, "n", x3[:, n % 2, :], n, "n_xT")
                if step.has("C"):
                    pool.wait_ge(e1_ready, step.done(p + 1))
                    pool.wait_ge(mask_ready, step.done(p + 1))
                    if p >= 1:
                        t.used(pool, step, f"c_t{NT - 1}", back=1)
                    pool.tensor_tensor(p1[:, :], e1[:, :], mask[:, :], ALU.mult).then_inc(p1_ready, 1)
                if step.has("E"):
                    heads_out(step, "e", e)
                if step.has("Q"):
                    norm(step, "q", x2[:, q % 2, :], q, "q_xT")
                if step.has("A"):
                    pool.wait_ge(nmax_ready, step.done(a + 1))
                    if a >= 1:
                        t.used(pool, step, f"e_t{NT - 1}")
                    pool.tensor_tensor(heads(e0[:, :]), heads(s0[:, :]),
                                       nmax[:, a % 2, :].unsqueeze(2).to_broadcast([P, H, CTX]), ALU.add)\
                        .then_inc(s0_shifted, 1)
                if step.has("F"):
                    norm(step, "f", x1[:, f % 2, :], f)
                if step.has("C"):
                    heads_out(step, "c", p)
                if step.has("F"):
                    pool.wait_ge(actA_ready, step.done(f + 1))
                    if f == 0:
                        pool.wait_ge(w_chain, 5)
                    if f >= 1:
                        pool.wait_ge(hA_ready, step.done(f))
                    scale = amax[:, f % 2, 2:3]
                    pool.tensor_tensor(cub[:, 0:1], scale, scale, ALU.mult).then_inc(cub_chain, 1)
                    pool.tensor_tensor(cub[:, 1:2], scale, wcub[:, 1:2], ALU.mult).then_inc(cub_chain, 1)
                    pool.wait_ge(cub_chain, step.done(f + 1, 2))
                    pool.tensor_tensor(cub[:, 2:3], cub[:, 0:1], cub[:, 1:2], ALU.mult).then_inc(cub_ready, 1)
                    g.landed(pool, step, "f_g")
                    u.landed(pool, step, "f_u")
                    pool.tensor_tensor(prod[:, :], relu_g[:, :], up_s[:, :], ALU.mult).then_inc(prod_ready, 1)
                    if f >= 1:
                        pool.wait_ge(hq_ready, step.done(f))
                    pool.wait_ge(prod_ready, step.done(f + 1))
                    pool.tensor_tensor(hid[:, :], prod[:, :], relu_g[:, :], ALU.mult).then_inc(hid_ready, 1)

            def block_keys(layer, b):
                pool.tensor_tensor(heads(KB[layer][:, b * HJ:(b + 1) * HJ]),
                                   KT[layer][:, b * CTX:(b + 1) * CTX].unsqueeze(1).to_broadcast([P, H, CTX]),
                                   part("hmask").unsqueeze(2).to_broadcast([P, H, CTX]), ALU.mult).then_inc(kb_ready, 1)

            def split_rows():
                n = 0
                whole = row_s[:, :]
                for i in range(ROW_PARTS):
                    part_ = row_part[:, i, :]
                    pool.tensor_tensor(part_, whole, row_zero[:, :], ALU.add).then_inc(row_split, 1)
                    n += 1
                    pool.wait_ge(row_split, n)
                    pool.tensor_tensor(row_own[:, i, :], part_,
                                       ident[0:ROW_PARTS, i:i + 1].to_broadcast([ROW_PARTS, ROW_W]), ALU.mult)\
                        .then_inc(row_split, 1)
                    n += 1
                    if i < ROW_PARTS - 1:
                        pool.tensor_tensor(row_rest[:, i, :], whole, part_, ALU.subtract)\
                            .then_inc(row_split, 1)
                        n += 1
                        whole = row_rest[:, i, :]
                        pool.wait_ge(row_split, n)
                pool.wait_ge(row_split, n)
                pool.tensor_tensor(row_bf[:, 0, :], row_own[:, 0, :], row_own[:, 1, :], ALU.add)\
                    .then_inc(row_split, 1)
                pool.wait_ge(row_split, n + 1)
                pool.tensor_tensor(row_bf[:, 1, :], row_bf[:, 0, :], row_own[:, 2, :], ALU.add)\
                    .then_inc(row_split, 1)

            pool.wait_ge(consts_set, 6)
            pool.wait_ge(pa_in, 16)
            pool.wait_ge(row_in, 16)
            split_rows()
            step_(Step(FIRST))
            pool.wait_ge(w_summed, 5)
            pool.partition_all_reduce(wtot[:, 0:3], wsum[:, 0:3], P, RADD).then_inc(w_totalled, 1)
            pool.partition_all_reduce(wtot[:, 3:5], wsum[:, 3:5], P, RMAX).then_inc(w_totalled, 1)
            s.landed(pool, setup1, "keys1")
            for b in range(1, B):
                block_keys(0, b)
                block_keys(1, b)
            middle_and_end(pool, step_)

        @block.scalar
        def _(act):
            def keys_values(layer, setup, bias):
                keys = s.see(act, setup, f"keys{layer}")
                act.activation(KT[layer][:, :], keys[:, 0:B * CTX], ACT.Identity, bias=bias).then_inc(s.out, 1)
                act.activation(values_of(layer)[:, :, :, DH], part("vmask").unsqueeze(1).to_broadcast([P, B, WC * WH]),
                               ACT.Copy).then_inc(ctx3_ready, 1)

            def step_(step):
                c = step.c
                a, e, f, d, q, p, n = (c + AT[k] for k in "AEFDQCN")

                def out(where, name, dst, fn=ACT.Copy, width=P, **kw):
                    product = where.see(act, step, name)
                    act.activation(dst, product[0:dst.shape[0], 0:width], fn, **kw).then_inc(where.out, 1)

                def scores_out(k, i, dst):
                    out(s, f"{k}_s{i}", dst[:, i * SC:(i + 1) * SC], width=SC, scale=ISQ)

                def gelu_out(where, name, half):
                    product = where.see(act, step, name)
                    for k in range(2 * half, 2 * half + 2):
                        ins = act.activation(hT[:, k, :], product[:, k % 2 * 2 * P:(k % 2 + 1) * 2 * P], ACT.Gelu,
                                             bias=part("bfc")[:, k:k + 1])
                    ins.then_inc(where.out, 1)

                def weights_out(k, i):
                    end = min((i + 1) * TURN, WC)
                    out(t, f"{k}_t{i}", pT[k][:, i * TURN * P:end * P], width=(end - i * TURN) * P)

                def heads_out(k, tile):
                    if tile >= 1:
                        act.wait_ge(on_ready[k], step.done(tile))
                        act.sem_inc(gate, 1)
                    out(o, f"{k}_o", osb[k][:, :], width=H * VW)

                if step.has("E"):
                    weights_out("e", 0)
                    weights_out("e", 1)
                if step.has("C"):
                    act.wait_ge(top_ready, step.done(p + 1, H))
                    if p >= 1:
                        act.wait_ge(p1_ready, step.done(p))
                    act.activation(mask[:, :], rest[p % 2][:, :], ACT.Relu, bias=-0.5, scale=1.0 / TAKEN)\
                       .then_inc(mask_ready, 1)
                if step.has("E"):
                    weights_out("e", 2)
                if step.has("A"):
                    out(m, "a_xT", xT["a"][:, :])
                if step.has("D"):
                    act.wait_ge(hA_ready, step.done(d + 1))
                    act.activation(hq[:, :], hid[:, :], ACT.Copy, scale=hA[:, d % 2:d % 2 + 1], bias=ROUND)\
                       .then_inc(hq_ready, 1)
                if step.has("A"):
                    out(m, "a_q", qT["a"][:, :], ACT.Identity, bias=part("bq0"))
                if step.has("D"):
                    out(g, "d_hT", hqT[:, :], ACT.Copy, width=FF, bias=-ROUND)
                if step.has("C"):
                    act.wait_ge(sm1_ready, step.done(p + 1))
                    act.activation(e1[:, :], sm1[:, :], ACT.Exp).then_inc(e1_ready, 1)
                if step.has("A"):
                    if a >= 1:
                        act.wait_ge(s0_shifted, step.done(a))
                        act.sem_inc(gate, 1)
                    scores_out("a", 0, s0)
                if step.has("E"):
                    heads_out("e", e)
                if step.has("A"):
                    scores_out("a", 1, s0)
                if step.has("N"):
                    out(m, "n_xT", x4T[:, n % 2, :])
                if step.has("A"):
                    scores_out("a", 2, s0)
                    scores_out("a", 3, s0)
                if step.has("E"):
                    out(m, "e_oT", oT["e"][:, :], ACT.Identity, bias=part("bv0"))
                if step.has("C"):
                    weights_out("c", 0)
                if step.has("E"):
                    if e >= 2:
                        u.landed(act, step, "d_down", back=1)
                        act.sem_inc(gate, 1)
                    out(m, "e_out", x1[:, e % 2, :])
                if step.has("G"):
                    gelu_out(g, "g_h0", 0)
                if step.has("C"):
                    weights_out("c", 1)
                if step.has("Q"):
                    out(m, "q_xT", xT["q"][:, :])
                if step.has("G"):
                    gelu_out(u, "g_h1", 1)
                if step.has("Q"):
                    out(m, "q_q", qT["q"][:, :], ACT.Identity, bias=part("bq1"))
                if step.has("C"):
                    weights_out("c", 2)
                if step.has("F"):
                    act.wait_ge(actA_ready, step.done(f + 1))
                    act.activation(yq[:, :], cen["f"][:, f % 2, :], ACT.Copy, scale=actA[:, f % 2:f % 2 + 1], bias=ROUND)\
                       .then_inc(yq_ready, 1)
                if step.has("C"):
                    heads_out("c", p)
                if step.has("F"):
                    out(m, "f_yT", yqT[:, :], ACT.Copy, bias=-ROUND)
                if step.has("Q"):
                    if q >= 2:
                        act.wait_ge(sm1_ready, step.done(q - 1))
                        act.sem_inc(gate, 1)
                    scores_out("q", 0, s1[q % 2])
                if step.has("F"):
                    if f >= 1:
                        act.wait_ge(hid_ready, step.done(f))
                        act.sem_inc(gate, 1)
                    out(g, "f_g", relu_g[:, :], ACT.Relu, width=FF)
                    out(u, "f_u", up_s[:, :], width=FF)
                if step.has("Q"):
                    scores_out("q", 1, s1[q % 2])
                    scores_out("q", 2, s1[q % 2])
                if step.has("C"):
                    out(m, "c_oT", oT["c"][:, :], ACT.Identity, bias=part("bv1"))
                if step.has("Q"):
                    scores_out("q", 3, s1[q % 2])
                if step.has("A"):
                    act.wait_ge(s0_shifted, step.done(a + 1))
                    act.activation(e0[:, :], e0[:, :], ACT.Exp).then_inc(e0_ready, 1)
                if step.has("G"):
                    gg = (c - 3) // 2
                    if gg >= 1:
                        act.wait_ge(y_stored, step.pairs(gg, 16))
                        act.sem_inc(gate, 1)
                    product = u.see(act, step, "g_out")
                    act.activation(y[:, :, :], product[:, 0:2 * D].rearrange("p (i d) -> p i d", i=2), ACT.Copy)\
                       .then_inc(u.out, 1)
                if step.has("C"):
                    out(m, "c_out", x3[:, p % 2, :])

            act.wait_ge(pa_in, 16)
            act.activation(ctx3[:, :].rearrange("p (b r j) -> p b r j", r=3, j=CTX),
                           part("ctx").rearrange("p (b j) -> p b j", j=CTX).unsqueeze(2).to_broadcast([P, B, 3, CTX]),
                           ACT.Copy).then_inc(ctx3_ready, 1)
            keys_values(0, setup0, part("bk0"))
            step_(Step(FIRST))
            keys_values(1, setup1, part("bk1"))
            middle_and_end(act, step_)

        @block.tensor
        def _(pe):
            def keys_values(layer, setup):
                keys = s.take(pe, setup, f"keys{layer}")
                pe.matmul(keys[:, 0:B * CTX], part(f"wk{layer}"), part("ctx"), start=True, stop=True)\
                  .then_inc(s.full, 1)
                pe.wait_ge(ctx3_ready, 1)
                for half in range(2):
                    values = t.take(pe, setup, f"v{layer}_{half}")
                    for b in range(2 * half, 2 * half + 2):
                        for i in range(WC):
                            at = (b % 2 * WC + place(i)) * WH * DH
                            tokens = b * REP + start(i) % CTX
                            ins = pe.matmul(values[:, at:at + WH * DH], ctx3[:, tokens:tokens + P],
                                            part(f"wv{layer}")[:, first_head(i) * DH:(first_head(i) + WH) * DH],
                                            start=True, stop=True)
                    ins.then_inc(t.full, 1)

            def transpose(step, name, src):
                dst = m.take(pe, step, name)
                pe.transpose(dst[:, 0:P], src, ident).then_inc(m.full, 1)

            def project(step, name, k, w):
                dst = m.take(pe, step, name)
                m.landed(pe, step, f"{name[0]}_xT")
                pe.matmul(dst[:, 0:P], part(w), xT[k][:, :], start=True, stop=True).then_inc(m.full, 1)

            def scores(step, k, layer, tile, i):
                dst = s.take(pe, step, f"{k}_s{i}")
                keys = KB[layer][:, bass.ds(step.batch(tile) * HJ + i * SC, SC)]
                pe.matmul(dst[:, 0:SC], qT[k][:, :], keys, start=True, stop=True).then_inc(s.full, 1)

            def turn_weights(step, k, i, src):
                dst = t.take(pe, step, f"{k}_t{i}")
                for n in range(i * TURN, min((i + 1) * TURN, WC)):
                    ins = pe.transpose(dst[:, n % TURN * P:(n % TURN + 1) * P], src[:, start(n):start(n) + P], ident)
                ins.then_inc(t.full, 1)

            def weigh(step, k, layer, tile, i):
                b = step.batch(tile)
                dst = o.take(pe, step, f"{k}_o") if i == 0 else o.slot(step, f"{k}_o")
                t.landed(pe, step, f"{k}_t{i}")
                for n in range(i * TURN, min((i + 1) * TURN, WC)):
                    heads_ = (first_head(n), first_head(n) + WH) if n else (0, H)
                    ins = pe.matmul(dst[:, heads_[0] * VW:heads_[1] * VW], pT[k][:, n * P:(n + 1) * P],
                                    V[layer][:, bass.ds(b * VB_W + place(n) * WH * VW, (heads_[1] - heads_[0]) * VW)],
                                    start=(n == 0), stop=(n == WC - 1))
                if i == NT - 1:
                    ins.then_inc(o.full, 1)

            def residual(step, name, k, w, bias, x):
                dst = m.take(pe, step, name)[:, 0:D]
                pe.matmul(dst, oT[k][:, :], part(w), start=True, stop=False)
                pe.matmul(dst, ones[:, :], row(bias), start=False, stop=False)
                pe.matmul(dst, ident, x, start=False, stop=True).then_inc(m.full, 1)

            def hidden(step, where, name, half):
                dst = where.take(pe, step, name)
                for k in range(2 * half, 2 * half + 2):
                    ins = pe.matmul(dst[:, k % 2 * 2 * P:(k % 2 + 1) * 2 * P], fcW[:, k * P:(k + 1) * P],
                                    x4T[:, :, :].rearrange("p i t -> p (i t)"), start=True, stop=True)
                ins.then_inc(where.full, 1)

            def step_(step):
                a, e, f, d, q, p, n = (step.c + AT[k] for k in "AEFDQCN")
                if step.has("E"):
                    pe.wait_ge(e0_ready, step.done(e + 1))
                    turn_weights(step, "e", 0, e0)
                    turn_weights(step, "e", 1, e0)
                    weigh(step, "e", 0, e, 0)
                    turn_weights(step, "e", 2, e0)
                if step.has("A"):
                    pe.wait_ge(ln["a"]["normed"], step.done(a + 1))
                    transpose(step, "a_xT", xn["a"][:, :])
                if step.has("E"):
                    weigh(step, "e", 0, e, 1)
                if step.has("A"):
                    project(step, "a_q", "a", "wq0")
                if step.has("D"):
                    pe.wait_ge(hq_ready, step.done(d + 1))
                    dst = g.take(pe, step, "d_hT")
                    for k in range(FC):
                        ins = pe.transpose(dst[:, k * P:(k + 1) * P], hq[:, k * P:(k + 1) * P], ident)
                    ins.then_inc(g.full, 1)
                if step.has("A"):
                    if a == 0:
                        pe.wait_ge(kb_ready, 1)
                    m.landed(pe, step, "a_q")
                    scores(step, "a", 0, a, 0)
                if step.has("E"):
                    weigh(step, "e", 0, e, 2)
                if step.has("D"):
                    dst = u.take(pe, step, "d_down")
                    g.landed(pe, step, "d_hT")
                    for k in range(FC):
                        ins = pe.matmul(dst[:, 0:D], hqT[:, k * P:(k + 1) * P], downQ[:, k * D:(k + 1) * D],
                                        start=(k == 0), stop=(k == FC - 1))
                    ins.then_inc(u.full, 1)
                if step.has("A"):
                    scores(step, "a", 0, a, 1)
                if step.has("N"):
                    pe.wait_ge(ln["n"]["normed"], step.done(n + 1))
                    transpose(step, "n_xT", xn["n"][:, :])
                if step.has("A"):
                    scores(step, "a", 0, a, 2)
                    scores(step, "a", 0, a, 3)
                if step.has("E"):
                    pe.wait_ge(on_ready["e"], step.done(e + 1))
                    transpose(step, "e_oT", on["e"][:, :])
                if step.has("G"):
                    m.landed(pe, step, "n_xT")
                    hidden(step, g, "g_h0", 0)
                if step.has("C"):
                    pe.wait_ge(p1_ready, step.done(p + 1))
                    turn_weights(step, "c", 0, p1)
                if step.has("E"):
                    if e == 0:
                        pe.wait_ge(row_split, 3 * ROW_PARTS + 1)
                    residual(step, "e_out", "e", "wo0", "bo0", xin[:, e % 2, :])
                if step.has("G"):
                    hidden(step, u, "g_h1", 1)
                if step.has("C"):
                    turn_weights(step, "c", 1, p1)
                if step.has("Q"):
                    pe.wait_ge(ln["q"]["normed"], step.done(q + 1))
                    transpose(step, "q_xT", xn["q"][:, :])
                if step.has("C"):
                    weigh(step, "c", 1, p, 0)
                if step.has("Q"):
                    project(step, "q_q", "q", "wq1")
                if step.has("C"):
                    turn_weights(step, "c", 2, p1)
                    weigh(step, "c", 1, p, 1)
                    weigh(step, "c", 1, p, 2)
                if step.has("F"):
                    pe.wait_ge(yq_ready, step.done(f + 1))
                    transpose(step, "f_yT", yq[:, :])
                if step.has("Q"):
                    if q == 0:
                        pe.wait_ge(kb_ready, 2 * B)
                    m.landed(pe, step, "q_q")
                    scores(step, "q", 1, q, 0)
                if step.has("F"):
                    m.landed(pe, step, "f_yT")
                    if f == 0:
                        pe.wait_ge(w_ready, 3)
                    for where, name, w in ((g, "f_g", gateQ), (u, "f_u", upQ)):
                        dst = where.take(pe, step, name)
                        pe.matmul(dst[:, :], yqT[:, :], w[:, :], start=True, stop=True).then_inc(where.full, 1)
                if step.has("Q"):
                    scores(step, "q", 1, q, 1)
                    scores(step, "q", 1, q, 2)
                if step.has("C"):
                    pe.wait_ge(on_ready["c"], step.done(p + 1))
                    transpose(step, "c_oT", on["c"][:, :])
                if step.has("Q"):
                    scores(step, "q", 1, q, 3)
                if step.has("G"):
                    g.landed(pe, step, "g_h0")
                    dst = u.take(pe, step, "g_out")
                    for i in range(2):
                        for k in range(FC):
                            pe.matmul(dst[:, i * D:(i + 1) * D], hT[:, k, i * P:(i + 1) * P], projW[:, k * D:(k + 1) * D],
                                      start=(k == 0), stop=False)
                        pe.matmul(dst[:, i * D:(i + 1) * D], ones[:, :], row("bproj"), start=False, stop=False)
                        ins = pe.matmul(dst[:, i * D:(i + 1) * D], ident, x3[:, i, :], start=False, stop=True)
                    ins.then_inc(u.full, 1)
                if step.has("C"):
                    pe.wait_ge(x2_kept[p % 2], step.loaded(p))
                    residual(step, "c_out", "c", "wo1", "bo1", x2keep[:, p % 2, :])

            pe.wait_ge(pa_in, 16)
            pe.wait_ge(consts_set, 1)
            keys_values(0, setup0)
            step_(Step(FIRST))
            pe.wait_ge(pc_in, 16)
            keys_values(1, setup1)
            pe.wait_ge(r16_in, 16)
            pe.matmul(g.take(pe, setup1, "lora_fc")[:, :], part("afc"), part("bfcT"), start=True, stop=True)\
              .then_inc(g.full, 1)
            dst = u.take(pe, setup1, "lora_proj")
            for k in range(FC):
                ins = pe.matmul(dst[:, k * D:(k + 1) * D], part("aproj")[:, k * P:(k + 1) * P], part("bprojT"),
                                start=True, stop=True)
            ins.then_inc(u.full, 1)
            t.landed(pe, setup1, "v1_1")
            middle_and_end(pe, step_)

        @block.sync
        def _(sp):
            x_t = x.rearrange("(t p) d -> t p d", p=P)
            out_g = out.rearrange("(g i p) d -> g p i d", i=2, p=P)

            def step_(step):
                c = step.c
                if c >= FIRST + 1:
                    sp.wait_ge(dve_over, step.plus(c - FIRST, 2))
                    sp.sem_inc(gate, 1)
                    sp.wait_ge(dve_step[(c - 1) % 2], dve_counts[standing_for(c - 1)])
                    sp.sem_inc(gate, 1)
                    sp.sem_clear(dve_step[(c - 1) % 2])
                    sp.sem_inc(dve_cleared, 1)
                if step.has("T"):
                    u.landed(sp, step, "d_down", back=1)
                    if c >= 2:
                        sp.sem_inc(gate, 1)
                        m.used(sp, step, "c_out", back=1)
                    sp.dma_start(x2keep[:, c % 2, :], x2[:, c % 2, :]).then_inc(x2_kept[c % 2], 16)
                if step.has("L"):
                    tile = c + AT["L"]
                    if tile >= 2:
                        m.used(sp, step, "e_out")
                    sp.dma_start(xin[:, tile % 2, :], x_t[step.plus(tile, 2)]).then_inc(x_in[tile % 2], 16)
                if step.has("G"):
                    gg = (c - 3) // 2
                    u.landed(sp, step, "g_out")
                    sp.dma_start(out_g[step.pairs(gg, 1)], y[:, :, :]).then_inc(y_stored, 16)

            sp.dma_start(xin[:, 0, :], x_t[0]).then_inc(x_in[0], 16)
            sp.dma_start(pa_s[:, :], pa).then_inc(pa_in, 16)
            sp.dma_start(row_s[:, :], rows).then_inc(row_in, 16)
            step_(Step(FIRST))
            sp.dma_start(pb_s[:, :], pb).then_inc(pb_in, 16)
            sp.dma_start(pc_s[:, :], pc).then_inc(pc_in, 16)
            sp.dma_start(r16_s[:, :], r16).then_inc(r16_in, 16)
            middle_and_end(sp, step_)
            sp.wait_ge(y_stored, 16 * (TILES // 2))


DUE = {"a_stats": 0, "d_hidden": 2, "n_stats": 12, "d_residual": 33, "e_recip": 38,
       "a_max": 50, "f_stats": 66, "f_scale": 76, "c_recip": 94}


def kernel(x, ctx_1024, **w):
    import numpy as np
    import concourse.bacc as bacc
    from concourse.bass_utils import run_bass_kernel_spmd

    w = {k: np.asarray(v) for k, v in w.items()}
    x, ctx_1024 = np.asarray(x), np.asarray(ctx_1024)

    def col(v):
        return v.reshape(-1, P).T

    def chunked(v):
        return v.T.reshape(FC, P, D).transpose(1, 0, 2).reshape(P, FF)

    dt = x.dtype
    ident = np.eye(P, dtype=dt)
    hmask = np.repeat(np.eye(H, dtype=dt), DH, axis=0)
    ctxT = ctx_1024.reshape(B * CTX, D).T
    vmask = np.zeros((P, WC, WH), dt)
    for i in range(WC):
        for r in range(P):
            head = (start(i) + r) // CTX - first_head(i)
            if start(i) + r >= i * P:
                vmask[r, place(i), head] = 1
    pa = np.concatenate([ident, hmask, col(w["L0_xattn_b_q"]), col(w["L0_xattn_b_k"]), col(w["L0_xattn_b_v"]),
                         vmask.reshape(P, WC * WH), w["L0_xattn_w_q"].T,
                         w["L0_xattn_w_k"].T, w["L0_xattn_w_v"].T, w["L0_xattn_w_o"].T, ctxT], axis=1)
    pb = np.concatenate([w["L0_ffn_w_gate"].T, w["L0_ffn_w_up"].T, chunked(w["L0_ffn_w_down"])], axis=1)
    pc = np.concatenate([w["L1_xattn_Wq"].T, w["L1_xattn_Wk"].T, w["L1_xattn_Wv"].T, w["L1_xattn_Wo"].T,
                         col(w["L1_xattn_bq"]), col(w["L1_xattn_bk"]), col(w["L1_xattn_bv"]), col(w["L1_ffn_b_fc"]), w["L1_ffn_W_fc"].T,
                         chunked(w["L1_ffn_W_proj"])], axis=1)
    rows = np.concatenate([w["L0_xattn_b_o"], w["L1_xattn_bo"],
                           w["L1_ffn_b_proj"]])[None, :].repeat(ROW_PARTS, axis=0)
    r16 = np.concatenate([w["L1_ffn_A_fc"], w["L1_ffn_B_fc"].T, w["L1_ffn_A_proj"], w["L1_ffn_B_proj"].T], axis=1)
    arrays = {"x": x.reshape(B * S, D), "pa": pa, "pb": pb, "pc": pc, "rows": rows, "r16": r16}
    arrays = {f"in_{k}": np.ascontiguousarray(v) for k, v in arrays.items()}

    nc = bacc.Bacc("TRN2", target_bir_lowering=False, num_devices=1)
    args = [nc.dram_tensor(k, v.shape, mybir.dt.from_np(v.dtype), kind="ExternalInput").ap() for k, v in arrays.items()]
    out = nc.dram_tensor("out_y", (B * S, D), F32, kind="ExternalOutput").ap()
    build(nc, *args, out)
    r = run_bass_kernel_spmd(nc, [arrays], core_ids=[0])
    return r.results[0]["out_y"].reshape(B, S, D)
```

```python
from contextlib import ExitStack

import concourse.bass as bass
from concourse import mybir

F32 = mybir.dt.float32
BF16 = mybir.dt.bfloat16
ALU = mybir.AluOpType
ACT = mybir.ActivationFunctionType
X = mybir.AxisListType.X
RMAX = bass.bass_isa.ReduceOp.max
RADD = bass.bass_isa.ReduceOp.add

B, S, D = 4, 512, 128
CTX = 77
H = 16
DH = D // H
FF = 512
FC = FF // D
RANK = 16
P = 128
TILES = B * S // P
TPB = S // P
HC = 4
NCH = H // HC
SC = HC * CTX
HJ = H * CTX
VW = DH + 1
WC = -(-HJ // P)
WH = 3
TURN = 4
NT = -(-WC // TURN)
VB_W = WC * WH * VW + (H - WH) * VW
REP = 3 * CTX
ROW_PARTS = 3
ROUNDS = 4
LN_EPS = 1e-5
Q_EPS = 1e-5
LORA_SCALE = 2.0
ROUND = 12582912.0
TAKEN = -float(2 ** 120)
ISQ = float(DH) ** -0.5

def start(i):
    return min(i * P, HJ - P)


def first_head(i):
    return min(start(i) // CTX, H - WH)


def place(i):
    return (i - 1) % WC


PA = {}
PB = {}
PC = {}
ROW = {}
R16 = {}


def _lay(table, *parts):
    at = 0
    for name, width in parts:
        table[name] = (at, at + width)
        at += width
    return at


PA_W = _lay(PA, ("ident", P), ("hmask", H), ("bq0", 1), ("bk0", 1), ("bv0", 1), ("vmask", WC * WH), ("wq0", D), ("wk0", D), ("wv0", D), ("wv1", D), ("wo0", D),
            ("ctx", B * CTX))
PB_W = _lay(PB, ("gate", FF), ("up", FF), ("down", FF))
PC_W = _lay(PC, ("wq1", D), ("wk1", D), ("wo1", D), ("bq1", 1), ("bk1", 1), ("bv1", 1), ("bfc", FC), ("fc", FF),
            ("proj", FF))
ROW_W = _lay(ROW, ("bo0", D), ("bo1", D), ("bproj", D))
R16_W = _lay(R16, ("afc", D), ("bfcT", FF), ("aproj", FF), ("bprojT", D))

AT = {"L": 4, "A": 3, "E": 2, "F": 2, "D": 1, "Q": 1, "T": 0, "C": -1, "N": -2}
FIRST, LAST = -AT["A"], TILES + 1
LOOP = (4, 5)
LOOPS = (TILES - AT["L"] - LOOP[0]) // 2


def has(stage, c):
    if stage == "G":
        return c % 2 == 1 and 3 <= c <= LAST
    return 0 <= c + AT[stage] < TILES


class Step:

    def __init__(self, c, j=None):
        self.c, self.j = c, j

    def has(self, stage):
        return has(stage, self.c)

    def plus(self, fixed, per_pair):
        return fixed if self.j is None or per_pair == 0 else self.j * per_pair + fixed

    def done(self, tile, per_tile=1, more=0):
        return self.plus(per_tile * tile + more, 2 * per_tile)

    def loaded(self, tile):
        return self.plus(16 * (tile // 2 + 1), 16)

    def pairs(self, g, per_pair=1, more=0):
        return self.plus(per_pair * g + more, per_pair)

    def batch(self, tile):
        if self.j is None:
            return tile // TPB
        return (self.j + tile // 2) // (TPB // 2)


def standing_for(c):
    return LOOP[c % 2] if LOOP[0] <= c < LOOP[0] + 2 * LOOPS else c


SETUPS = [f"setup{i}" for i in range(7)]
ORDER = [key for i, c in enumerate(range(FIRST, LAST + 1)) for key in SETUPS[i:i + 1] + [c]]
VALUES = ["setup1", "setup3", "setup4", "setup5"]
KEYS = {"setup3": [(0, 1)], "setup4": [(1, 1)], "setup5": [(0, 2), (1, 2)], "setup6": [(0, 3), (1, 3)]}


class Bank:

    def __init__(self, tensors, full, out, setups, names):
        self.tensors, self.full, self.out = tensors, full, out
        self.fixed = {key: setups.get(key, []) for key in SETUPS}
        self.names = names

    def users(self, key):
        if key in self.fixed:
            return self.fixed[key]
        return [n for n in self.names if has(n[0].upper(), key)]

    def turn(self, step, name, back=0):
        key = step.c if not back else step.c - back
        if step.j is not None:
            assert self.users(key) == self.users(key + 2)
        before = sum(len(self.users(k)) for k in ORDER[:ORDER.index(key)])
        return before + self.users(key).index(name), sum(len(self.users(k)) for k in LOOP)

    def slot(self, step, name):
        n, per_pair = self.turn(step, name)
        assert step.j is None or per_pair % len(self.tensors) == 0
        return self.tensors[n % len(self.tensors)]

    def take(self, pe, step, name):
        n, per_pair = self.turn(step, name)
        n -= len(self.tensors) - 1
        if n > 0:
            pe.wait_ge(self.out, step.plus(n, per_pair))
        return self.slot(step, name)

    def see(self, eng, step, name):
        n, per_pair = self.turn(step, name)
        eng.wait_ge(self.full, step.plus(n + 1, per_pair))
        return self.slot(step, name)

    def landed(self, eng, step, name, back=0):
        n, per_pair = self.turn(step, name, back)
        eng.wait_ge(self.out, step.plus(n + 1, per_pair))

    def used(self, eng, step, name, back=0):
        n, per_pair = self.turn(step, name, back)
        eng.wait_ge(self.full, step.plus(n + 1, per_pair))


def build(nc, x, pa, pb, pc, rows, r16, out):
    with ExitStack() as ctx:
        def sb(name, shape, dt=F32):
            return ctx.enter_context(nc.sbuf_tensor(name, shape, dt))

        def sem(name):
            return ctx.enter_context(nc.semaphore(name))

        pa_s, pb_s, pc_s = sb("pa_s", [P, PA_W]), sb("pb_s", [P, PB_W]), sb("pc_s", [P, PC_W])
        row_s, r16_s = sb("row_s", [ROW_PARTS, ROW_W]), sb("r16_s", [RANK, R16_W])

        def part(name):
            for tensor, table in ((pa_s, PA), (pb_s, PB), (pc_s, PC), (r16_s, R16)):
                if name in table:
                    return tensor[:, table[name][0]:table[name][1]]

        def row(name):
            return row_bf[:, 1, ROW[name][0]:ROW[name][1]]

        ident = part("ident")
        ones = sb("ones", [ROW_PARTS, P], BF16)
        row_part = sb("row_part", [ROW_PARTS, ROW_PARTS, ROW_W], BF16)
        row_rest = sb("row_rest", [ROW_PARTS, 2, ROW_W])
        row_own = sb("row_own", [ROW_PARTS, ROW_PARTS, ROW_W], BF16)
        row_zero = sb("row_zero", [ROW_PARTS, ROW_W])
        row_bf = sb("row_bf", [ROW_PARTS, 2, ROW_W], BF16)
        eps, mhalf = sb("eps", [P, 1]), sb("mhalf", [P, 1])
        wsum = sb("wsum", [P, 8])
        wtot = sb("wtot", [P, 8])
        wscale = sb("wscale", [P, 8])
        wrec = sb("wrec", [P, 8])
        wcub = sb("wcub", [P, 2])
        wtmp = sb("wtmp", [P, 2, FF])
        gateQ, upQ, downQ = (sb(n, [P, FF], BF16) for n in ("gateQ", "upQ", "downQ"))
        fcW, projW = sb("fcW", [P, FF]), sb("projW", [P, FF])
        KT = [sb(f"KT{l}", [P, B * CTX]) for l in range(2)]
        KB = [sb(f"KB{l}", [P, B * HJ]) for l in range(2)]
        ctx3 = sb("ctx3", [P, B * REP])
        v_raw = sb("v_raw", [P, 2, WC * 2 * WH * DH])
        V = [sb(f"V{l}", [P, B * VB_W]) for l in range(2)]

        xin = sb("xin", [P, 2, D])
        stats = {k: sb(f"stats_{k}", [P, 2, 6]) for k in "afqn"}
        mv = {k: sb(f"mv_{k}", [P, 2, 2]) for k in "afqn"}
        ve = {k: sb(f"ve_{k}", [P, 1]) for k in "afqn"}
        rstd = {k: sb(f"rstd_{k}", [P, 2]) for k in "afqn"}
        cen = {k: sb(f"cen_{k}", [P, 2, D]) for k in "afqn"}
        xn = {k: sb(f"xn_{k}", [P, D]) for k in "aqn"}
        xT = {k: sb(f"xT_{k}", [P, P]) for k in "aq"}
        qT = {k: sb(f"qT_{k}", [P, P]) for k in "aq"}
        s0, e0 = sb("s0", [P, HJ]), sb("e0", [P, HJ])
        nmax = sb("nmax", [P, 2, H])
        pT = {k: sb(f"pT_{k}", [P, WC * P]) for k in "ec"}
        osb = {k: sb(f"osb_{k}", [P, H * VW]) for k in "ec"}
        rden = {k: sb(f"rden_{k}", [P, 2, H]) for k in "ec"}
        on = {k: sb(f"on_{k}", [P, D]) for k in "ec"}
        oT = {k: sb(f"oT_{k}", [P, P]) for k in "ec"}
        x1, x2, x2keep, x3 = (sb(n, [P, 2, D]) for n in ("x1", "x2", "x2keep", "x3"))
        amax = sb("amax", [P, 2, 4])
        actA = sb("actA", [P, 2])
        yq, yqT = sb("yq", [P, P]), sb("yqT", [P, P], BF16)
        cub = sb("cub", [P, 3])
        relu_g, up_s, prod, hid = (sb(n, [P, FF]) for n in ("relu_g", "up_s", "prod", "hid"))
        hmax = sb("hmax", [P, 2, 4])
        hA, osc = sb("hA", [P, 2]), sb("osc", [P, 2])
        hq, hqT = sb("hq", [P, FF]), sb("hqT", [P, FF], BF16)
        s1 = [sb(f"s1_{i}", [P, HJ]) for i in range(2)]
        rest = [sb(f"rest_{i}", [P, HJ]) for i in range(2)]
        top = sb("top", [P, 2, H, ROUNDS, 8])
        sm1, e1, mask, p1 = (sb(n, [P, HJ]) for n in ("sm1", "e1", "mask", "p1"))
        x4T = sb("x4T", [P, 2, P])
        hT = sb("hT", [P, FC, 2 * P])
        y = sb("y", [P, 2, D])
        mark = sb("mark", [1, 2])

        pa_in, pb_in, pc_in, row_in, r16_in = (sem(n) for n in ("pa_in", "pb_in", "pc_in", "row_in", "r16_in"))
        consts_set, kb_ready, ctx3_ready = sem("consts_set"), sem("kb_ready"), sem("ctx3_ready")
        kb_rest, v_copied, v_masked = sem("kb_rest"), sem("v_copied"), sem("v_masked")
        row_split = sem("row_split")
        w_summed, w_totalled, w_chain, w_ready = (sem(n) for n in ("w_summed", "w_totalled", "w_chain", "w_ready"))
        x_in, x2_kept = [sem("x_in_even"), sem("x_in_odd")], [sem("x2_kept_even"), sem("x2_kept_odd")]
        y_stored = sem("y_stored")
        gate = sem("gate")
        dve_step = [sem("dve_step_even"), sem("dve_step_odd")]
        dve_over, dve_cleared = sem("dve_over"), sem("dve_cleared")
        ln = {k: {n: sem(f"{k}_{n}") for n in ("stats", "chain", "centred", "normed")} for k in "afqn"}
        nmax_ready, s0_shifted, e0_ready = sem("nmax_ready"), sem("s0_shifted"), sem("e0_ready")
        rden_ready = {k: sem(f"rden_ready_{k}") for k in "ec"}
        on_ready = {k: sem(f"on_ready_{k}") for k in "ec"}
        actA_ready, yq_ready, cub_chain, cub_ready = (sem(n) for n in ("actA_ready", "yq_ready", "cub_chain", "cub_ready"))
        prod_ready, hid_ready, hA_ready, hq_ready = (sem(n) for n in ("prod_ready", "hid_ready", "hA_ready", "hq_ready"))
        top_ready, sm1_ready, e1_ready, mask_ready, p1_ready = (
            sem(n) for n in ("top_ready", "sm1_ready", "e1_ready", "mask_ready", "p1_ready"))

        banks = [ctx.enter_context(nc.psum_tensor(f"bank{i}", [P, 512], F32)) for i in range(8)]

        def bank(name, tensors, setups, names):
            return Bank(tensors, sem(f"{name}_full"), sem(f"{name}_out"), setups, names)

        m = bank("m", [banks[0]], {},
                 ["a_xT", "a_q", "n_xT", "e_oT", "e_out", "q_xT", "q_q", "f_yT", "c_oT", "c_out"])
        o = bank("o", [banks[1]], {}, ["e_o", "c_o"])
        g = bank("g", [banks[2]], {"setup5": ["lora_fc"]}, ["d_hT", "g_h0", "f_g"])
        u = bank("u", [banks[3]], {"setup5": ["lora_proj"]}, ["d_down", "g_h1", "f_u", "g_out"])
        s = bank("s", banks[4:6], {"setup0": ["keys0"], "setup2": ["keys1"]}, [f"{k}_s{i}" for k in "aq" for i in range(NCH)])
        t = bank("t", banks[6:8], {setup: [f"v{b}"] for b, setup in enumerate(VALUES)},
                 [f"{k}_t{i}" for k in "ec" for i in range(NT)])
        setup0, setup2, setup5 = Step("setup0"), Step("setup2"), Step("setup5")

        def heads(ap, w=CTX):
            return ap.rearrange("p (h j) -> p h j", j=w)

        def values_of(layer):
            return V[layer][:, :].rearrange("p (b w) -> p b w", b=B)[:, :, 0:WC * WH * VW]\
                .rearrange("p b (k v) -> p b k v", v=VW)

        def all_steps(eng, step_, setup_):
            for i, c in enumerate(range(FIRST, LOOP[0])):
                if i < len(SETUPS):
                    setup_(SETUPS[i])
                step_(Step(c))
            with eng.Fori(0, LOOPS) as j:
                for c in LOOP:
                    step_(Step(c, j))
            for c in range(LOOP[0] + 2 * LOOPS, LAST + 1):
                step_(Step(c))

        block = ctx.enter_context(nc.Block())
        dve_counts = {}

        @block.vector
        def _(dve):
            dve.memset(ones[:, :], 1.0).then_inc(consts_set, 1)
            for l in range(2):
                dve.memset(V[l].rearrange("p (b w) -> p b w", b=B)[:, :, WC * WH * VW:], 0.0).then_inc(consts_set, 1)
            dve.memset(eps[:, :], LN_EPS).then_inc(consts_set, 1)
            dve.memset(mhalf[:, :], -0.5).then_inc(consts_set, 1)
            dve.memset(row_zero[:, :], 0.0).then_inc(consts_set, 1)

            class Own:

                def __init__(self, step):
                    self.sem, self.n = dve_step[step.c % 2], 0

                def out(self, ins):
                    self.n += 1
                    ins.then_inc(self.sem, 1)
                    return self.n

                def wait(self, n):
                    dve.wait_ge(self.sem, n)

            def ln_stats(own, step, k, src, tile):
                par = tile % 2
                if tile >= 2:
                    dve.wait_ge(ln[k]["normed"], step.done(tile - 1))
                n = own.out(dve.bn_stats(stats[k][:, par, :], src))
                yield
                own.wait(n)
                dve.bn_aggr(mv[k][:, par, :], stats[k][:, par, :]).then_inc(ln[k]["stats"], 1)

            def a_stats(own, step):
                a = step.c + AT["A"]
                dve.wait_ge(x_in[a % 2], step.loaded(a))
                yield from ln_stats(own, step, "a", xin[:, a % 2, :], a)

            def a_max(own, step):
                a = step.c + AT["A"]
                s.landed(dve, step, f"a_s{NCH - 1}")
                dve.tensor_reduce(nmax[:, a % 2, :], heads(s0[:, :]), X, ALU.max, negate=True).then_inc(nmax_ready, 1)

            def recip(step, k):
                tile = step.c + AT[k.upper()]
                o.landed(dve, step, f"{k}_o")
                dve.reciprocal(rden[k][:, tile % 2, :], heads(osb[k][:, :], VW)[:, :, DH]).then_inc(rden_ready[k], 1)

            def f_stats(own, step):
                f = step.c + AT["F"]
                m.landed(dve, step, "e_out")
                yield from ln_stats(own, step, "f", x1[:, f % 2, :], f)

            def f_scale(own, step):
                f = step.c + AT["F"]
                par = f % 2
                a_ = amax[:, par, :]
                dve.wait_ge(ln["f"]["centred"], step.done(f + 1))
                n = own.out(dve.tensor_reduce(a_[:, 0:1], cen["f"][:, par, :], X, ALU.max, apply_absolute_value=True))
                yield
                dve.wait_ge(ln["f"]["normed"], step.done(f + 1))
                own.wait(n)
                n = own.out(dve.tensor_tensor(a_[:, 1:2], a_[:, 0:1], rstd["f"][:, par:par + 1], ALU.mult))
                yield
                own.wait(n)
                n = own.out(dve.tensor_scalar(a_[:, 2:3], a_[:, 1:2], Q_EPS, 1.0 / 127.0, ALU.max, ALU.mult))
                yield
                own.wait(n)
                n = own.out(dve.reciprocal(a_[:, 3:4], a_[:, 2:3]))
                yield
                own.wait(n)
                dve.tensor_tensor(actA[:, par:par + 1], a_[:, 3:4], rstd["f"][:, par:par + 1], ALU.mult)\
                   .then_inc(actA_ready, 1)

            def d_hidden_scale(own, step, kept):
                d = step.c + AT["D"]
                par = d % 2
                h_ = hmax[:, par, :]
                dve.wait_ge(hid_ready, step.done(d + 1))
                n = own.out(dve.tensor_reduce(h_[:, 0:1], hid[:, :], X, ALU.max, apply_absolute_value=True))
                yield
                dve.wait_ge(cub_ready, step.done(d + 1))
                own.wait(n)
                n = own.out(dve.tensor_tensor(h_[:, 1:2], h_[:, 0:1], cub[:, 2:3], ALU.mult))
                yield
                own.wait(n)
                n = own.out(dve.tensor_scalar(h_[:, 2:3], h_[:, 1:2], Q_EPS, 1.0 / 127.0, ALU.max, ALU.mult))
                yield
                own.wait(n)
                n = own.out(dve.reciprocal(h_[:, 3:4], h_[:, 2:3]))
                kept["osc"] = own.out(dve.tensor_tensor(osc[:, par:par + 1], h_[:, 2:3], wscale[:, 2:3], ALU.mult))
                yield
                own.wait(n)
                dve.tensor_tensor(hA[:, par:par + 1], h_[:, 3:4], cub[:, 2:3], ALU.mult).then_inc(hA_ready, 1)

            def d_residual(own, step, kept):
                d = step.c + AT["D"]
                par = d % 2
                product = u.see(dve, step, "d_down")
                if d >= 2:
                    dve.wait_ge(x2_kept[par], step.loaded(d - 2))
                    dve.wait_ge(ln["q"]["centred"], step.done(d - 1))
                own.wait(kept["osc"])
                dve.scalar_tensor_tensor(x2[:, par, :], product[:, 0:D], osc[:, par:par + 1], x1[:, par, :],
                                         ALU.mult, ALU.add).then_inc(u.out, 1)
                yield
                u.landed(dve, step, "d_down")
                yield from ln_stats(own, step, "q", x2[:, par, :], d)

            def n_stats(own, step):
                n = step.c + AT["N"]
                m.landed(dve, step, "c_out", back=1)
                yield from ln_stats(own, step, "n", x3[:, n % 2, :], n)

            def top_rounds(own, step):
                par = step.c % 2
                scores, marked = heads(s1[par][:, :]), heads(rest[par][:, :])
                for h0 in range(0, H, 8):
                    made = {}
                    for r in range(ROUNDS):
                        src = marked if r else scores
                        for h in range(h0, h0 + 8):
                            if r:
                                own.wait(made[h])
                            made[h] = own.out(dve.max(top[:, par, h, r, :], src[:, h, :]))
                            yield
                        for h in range(h0, h0 + 8):
                            own.wait(made[h])
                            ins = dve.match_replace(marked[:, h, :], top[:, par, h, r, :], src[:, h, :], TAKEN)
                            if r == ROUNDS - 1:
                                ins.then_inc(top_ready, 1)
                            else:
                                made[h] = own.out(ins)
                            yield

            def split_rows():
                dve.wait_ge(row_in, 16)
                n = 0
                whole = row_s[:, :]
                for i in range(ROW_PARTS):
                    part_ = row_part[:, i, :]
                    dve.tensor_tensor(part_, whole, row_zero[:, :], ALU.add).then_inc(row_split, 1)
                    n += 1
                    dve.wait_ge(row_split, n)
                    dve.tensor_tensor(row_own[:, i, :], part_,
                                       ident[0:ROW_PARTS, i:i + 1].to_broadcast([ROW_PARTS, ROW_W]), ALU.mult)\
                        .then_inc(row_split, 1)
                    n += 1
                    if i < ROW_PARTS - 1:
                        dve.tensor_tensor(row_rest[:, i, :], whole, part_, ALU.subtract)\
                            .then_inc(row_split, 1)
                        n += 1
                        whole = row_rest[:, i, :]
                        dve.wait_ge(row_split, n)
                dve.wait_ge(row_split, n)
                dve.tensor_tensor(row_bf[:, 0, :], row_own[:, 0, :], row_own[:, 1, :], ALU.add)\
                    .then_inc(row_split, 1)
                dve.wait_ge(row_split, n + 1)
                dve.tensor_tensor(row_bf[:, 1, :], row_bf[:, 0, :], row_own[:, 2, :], ALU.add)\
                    .then_inc(row_split, 1)

            def step_(step):
                c = step.c
                own = Own(step)
                if c >= FIRST + 2:
                    dve.wait_ge(dve_cleared, step.plus(c - FIRST - 1, 2))
                    dve.sem_inc(gate, 1)
                if step.has("T"):
                    s.landed(dve, step, f"q_s{NCH - 1}", back=1)
                    dve.sem_inc(gate, 1)
                    if c >= 2:
                        dve.wait_ge(mask_ready, step.done(c - 1))
                        dve.sem_inc(gate, 1)
                        dve.wait_ge(sm1_ready, step.done(c - 1))
                        dve.sem_inc(gate, 1)
                small, kept = [], {}
                parts = {
                    "A": {"a_stats": lambda: a_stats(own, step), "a_max": lambda: a_max(own, step)},
                    "E": {"e_recip": lambda: recip(step, "e")},
                    "F": {"f_stats": lambda: f_stats(own, step), "f_scale": lambda: f_scale(own, step)},
                    "D": {"d_hidden": lambda: d_hidden_scale(own, step, kept),
                          "d_residual": lambda: d_residual(own, step, kept)},
                    "C": {"c_recip": lambda: recip(step, "c")},
                    "N": {"n_stats": lambda: n_stats(own, step)},
                }
                for stage, group in parts.items():
                    if step.has(stage):
                        small += [(DUE[name], part_) for name, part_ in group.items()]
                if c == FIRST:
                    small.append((DUE["a_stats"] + 1, split_rows))
                small.sort(key=lambda due: due[0])
                begun = []
                for n, _ in enumerate(top_rounds(own, step) if step.has("T") else ()):
                    if begun and next(begun[0], "done") == "done":
                        begun.pop(0)
                    while small and small[0][0] <= n:
                        work = small.pop(0)[1]()
                        if work is not None and (begun or next(work, "done") != "done"):
                            begun.append(work)
                for work in begun:
                    for _ in work:
                        pass
                for _, part_ in small:
                    for _ in part_() or ():
                        pass
                dve.memset(mark[:, c % 2:c % 2 + 1], 0.0).then_inc(dve_over, 1)
                dve_counts[c] = own.n

            def block_keys(layer, b):
                dve.tensor_tensor(heads(KB[layer][:, b * HJ:(b + 1) * HJ]),
                                  KT[layer][:, b * CTX:(b + 1) * CTX].unsqueeze(1).to_broadcast([P, H, CTX]),
                                  part("hmask").unsqueeze(2).to_broadcast([P, H, CTX]), ALU.mult).then_inc(kb_ready, 1)

            def weight_scales():
                dve.wait_ge(pb_in, 16)
                for i, name in enumerate(("gate", "up", "down")):
                    dve.tensor_reduce(wsum[:, i:i + 1], part(name), X, ALU.add, apply_absolute_value=True)\
                       .then_inc(w_summed, 1)
                dve.wait_ge(pc_in, 16)
                for i, name in enumerate(("fc", "proj")):
                    dve.tensor_reduce(wsum[:, 3 + i:4 + i], part(name), X, ALU.max, apply_absolute_value=True)\
                       .then_inc(w_summed, 1)
                dve.wait_ge(w_totalled, 2)
                dve.tensor_scalar(wscale[:, 0:3], wtot[:, 0:3], 1.0 / (FF * D), Q_EPS, ALU.mult, ALU.max)\
                   .then_inc(w_chain, 1)
                dve.tensor_scalar(wscale[:, 3:5], wtot[:, 3:5], 1.0 / 127.0, None, ALU.mult).then_inc(w_chain, 1)
                dve.wait_ge(w_chain, 2)
                dve.reciprocal(wrec[:, 0:5], wscale[:, 0:5]).then_inc(w_chain, 1)
                dve.tensor_tensor(wcub[:, 0:1], wscale[:, 0:1], wscale[:, 0:1], ALU.mult).then_inc(w_chain, 1)
                dve.wait_ge(w_chain, 4)
                dve.tensor_tensor(wcub[:, 1:2], wcub[:, 0:1], wscale[:, 1:2], ALU.mult).then_inc(w_chain, 1)
                return 5

            def round_weights(chain):
                for i, (name, dst) in enumerate((("gate", gateQ), ("up", upQ), ("down", downQ))):
                    tmp = wtmp[:, i % 2, :]
                    if i == 2:
                        dve.wait_ge(w_ready, 1)
                    dve.tensor_scalar(tmp, part(name), wrec[:, i:i + 1], 1.0, ALU.mult, ALU.min).then_inc(w_chain, 1)
                    dve.wait_ge(w_chain, chain + 1)
                    dve.tensor_scalar(tmp, tmp, -1.0, ROUND, ALU.max, ALU.add).then_inc(w_chain, 1)
                    dve.wait_ge(w_chain, chain + 2)
                    dve.tensor_scalar(dst[:, :], tmp, -ROUND, None, ALU.add).then_inc(w_ready, 1)
                    chain += 2
                return chain

            def round_and_merge(chain):
                dve.wait_ge(w_ready, 3)
                for i, (name, where, user) in enumerate((("fc", g, "lora_fc"), ("proj", u, "lora_proj"))):
                    tmp = wtmp[:, i, :]
                    dve.tensor_scalar(tmp, part(name), wrec[:, 3 + i:4 + i], 127.0, ALU.mult, ALU.min)\
                       .then_inc(w_chain, 1)
                    dve.wait_ge(w_chain, chain + 1)
                    dve.tensor_scalar(tmp, tmp, -128.0, ROUND, ALU.max, ALU.add).then_inc(w_chain, 1)
                    dve.wait_ge(w_chain, chain + 2)
                    dve.tensor_scalar(tmp, tmp, -ROUND, wscale[:, 3 + i:4 + i], ALU.add, ALU.mult).then_inc(w_chain, 1)
                    chain += 3
                    product = where.see(dve, setup5, user)
                    dve.wait_ge(w_chain, chain)
                    dve.scalar_tensor_tensor((fcW, projW)[i][:, :], product[:, :], LORA_SCALE, tmp, ALU.mult, ALU.add)\
                       .then_inc(where.out, 1)

            def setup_(setup):
                if setup == "setup0":
                    dve.wait_ge(pa_in, 16)
                    s.landed(dve, setup0, "keys0")
                    block_keys(0, 0)
                if setup == "setup1":
                    round_weights(weight_scales())
                if setup == "setup2":
                    s.landed(dve, setup2, "keys1")
                    block_keys(1, 0)
                if setup == "setup5":
                    round_and_merge(5 + 2 * 3)

            all_steps(dve, step_, setup_)

        @block.gpsimd
        def _(pool):
            def norm(step, k, src, tile, turn=None, back=1):
                par = tile % 2
                pool.wait_ge(ln[k]["stats"], step.done(tile + 1))
                if k == "f" and tile >= 2:
                    pool.wait_ge(yq_ready, step.done(tile - 1))
                pool.tensor_tensor(cen[k][:, par, :], src, mv[k][:, par, 0:1].to_broadcast([P, D]), ALU.subtract)\
                    .then_inc(ln[k]["centred"], 1)
                pool.tensor_tensor(ve[k][:, :], mv[k][:, par, 1:2], eps[:, :], ALU.add).then_inc(ln[k]["chain"], 1)
                if turn is None:
                    pool.wait_ge(ln[k]["chain"], step.done(tile + 1))
                    pool.tensor_tensor(rstd[k][:, par:par + 1], ve[k][:, :], mhalf[:, :], ALU.pow)\
                        .then_inc(ln[k]["normed"], 1)
                    return
                pool.wait_ge(ln[k]["chain"], step.done(tile, 2, 1))
                pool.tensor_tensor(rstd[k][:, par:par + 1], ve[k][:, :], mhalf[:, :], ALU.pow)\
                    .then_inc(ln[k]["chain"], 1)
                pool.wait_ge(ln[k]["centred"], step.done(tile + 1))
                if tile >= 1:
                    m.used(pool, step, turn, back=back)
                pool.wait_ge(ln[k]["chain"], step.done(tile, 2, 2))
                pool.tensor_tensor(xn[k][:, :], cen[k][:, par, :], rstd[k][:, par:par + 1].to_broadcast([P, D]),
                                   ALU.mult).then_inc(ln[k]["normed"], 1)

            def heads_out(step, k, tile):
                pool.wait_ge(rden_ready[k], step.done(tile + 1))
                if tile >= 1:
                    m.used(pool, step, f"{k}_oT", back=1)
                pool.tensor_tensor(heads(on[k][:, :], DH), heads(osb[k][:, :], VW)[:, :, 0:DH],
                                   rden[k][:, tile % 2, :].unsqueeze(2).to_broadcast([P, H, DH]), ALU.mult)\
                    .then_inc(on_ready[k], 1)

            def step_(step):
                a, e, f, q, p, n = (step.c + AT[k] for k in "AEFQCN")
                if step.has("A"):
                    norm(step, "a", xin[:, a % 2, :], a, "a_xT")
                if step.has("C"):
                    pool.wait_ge(top_ready, step.done(p + 1, H))
                    if p >= 1:
                        pool.wait_ge(e1_ready, step.done(p))
                    pool.tensor_tensor(heads(sm1[:, :]), heads(s1[p % 2][:, :]),
                                       top[:, p % 2, :, 0, 0:1].to_broadcast([P, H, CTX]), ALU.subtract)\
                        .then_inc(sm1_ready, 1)
                if step.has("N"):
                    norm(step, "n", x3[:, n % 2, :], n, "n_xT")
                if step.has("C"):
                    pool.wait_ge(e1_ready, step.done(p + 1))
                    pool.wait_ge(mask_ready, step.done(p + 1))
                    if p >= 1:
                        t.used(pool, step, f"c_t{NT - 1}", back=1)
                    pool.tensor_tensor(p1[:, :], e1[:, :], mask[:, :], ALU.mult).then_inc(p1_ready, 1)
                if step.has("E"):
                    heads_out(step, "e", e)
                if step.has("Q"):
                    norm(step, "q", x2[:, q % 2, :], q, "q_xT")
                if step.has("A"):
                    pool.wait_ge(nmax_ready, step.done(a + 1))
                    if a >= 1:
                        t.used(pool, step, f"e_t{NT - 1}")
                    pool.tensor_tensor(heads(e0[:, :]), heads(s0[:, :]),
                                       nmax[:, a % 2, :].unsqueeze(2).to_broadcast([P, H, CTX]), ALU.add)\
                        .then_inc(s0_shifted, 1)
                if step.has("F"):
                    norm(step, "f", x1[:, f % 2, :], f)
                if step.has("C"):
                    heads_out(step, "c", p)
                if step.has("F"):
                    pool.wait_ge(actA_ready, step.done(f + 1))
                    if f == 0:
                        pool.wait_ge(w_chain, 5)
                    if f >= 1:
                        pool.wait_ge(hA_ready, step.done(f))
                    scale = amax[:, f % 2, 2:3]
                    pool.tensor_tensor(cub[:, 0:1], scale, scale, ALU.mult).then_inc(cub_chain, 1)
                    pool.tensor_tensor(cub[:, 1:2], scale, wcub[:, 1:2], ALU.mult).then_inc(cub_chain, 1)
                    pool.wait_ge(cub_chain, step.done(f + 1, 2))
                    pool.tensor_tensor(cub[:, 2:3], cub[:, 0:1], cub[:, 1:2], ALU.mult).then_inc(cub_ready, 1)
                    g.landed(pool, step, "f_g")
                    u.landed(pool, step, "f_u")
                    pool.tensor_tensor(prod[:, :], relu_g[:, :], up_s[:, :], ALU.mult).then_inc(prod_ready, 1)
                    if f >= 1:
                        pool.wait_ge(hq_ready, step.done(f))
                    pool.wait_ge(prod_ready, step.done(f + 1))
                    pool.tensor_tensor(hid[:, :], prod[:, :], relu_g[:, :], ALU.mult).then_inc(hid_ready, 1)

            def block_keys(layer, b):
                pool.tensor_tensor(heads(KB[layer][:, b * HJ:(b + 1) * HJ]),
                                   KT[layer][:, b * CTX:(b + 1) * CTX].unsqueeze(1).to_broadcast([P, H, CTX]),
                                   part("hmask").unsqueeze(2).to_broadcast([P, H, CTX]), ALU.mult).then_inc(kb_rest, 1)

            def setup_(setup):
                if setup == "setup0":
                    pool.wait_ge(consts_set, 6)
                    pool.wait_ge(pa_in, 16)
                if setup == "setup1":
                    pool.wait_ge(w_summed, 5)
                    pool.partition_all_reduce(wtot[:, 0:3], wsum[:, 0:3], P, RADD).then_inc(w_totalled, 1)
                    pool.partition_all_reduce(wtot[:, 3:5], wsum[:, 3:5], P, RMAX).then_inc(w_totalled, 1)
                if setup == "setup3":
                    s.landed(pool, setup2, "keys1")
                for layer, b in KEYS.get(setup, []):
                    block_keys(layer, b)
                for b, when in enumerate(VALUES):
                    if when == setup:
                        pool.wait_ge(v_copied, b + 1)
                        raw = v_raw[:, b % 2, :].rearrange("p (i l k d) -> p l i k d", l=2, k=WH, d=DH)
                        for layer in range(2):
                            pool.tensor_tensor(
                                values_of(layer)[:, b, :, :].rearrange("p (i k) v -> p i k v", k=WH)[:, :, :, 0:DH],
                                raw[:, layer, :, :, :],
                                part("vmask").rearrange("p (i k) -> p i k", k=WH).unsqueeze(3)
                                .to_broadcast([P, WC, WH, DH]), ALU.mult).then_inc(v_masked, 1)

            all_steps(pool, step_, setup_)

        @block.scalar
        def _(act):
            def step_(step):
                c = step.c
                a, e, f, d, q, p, n = (c + AT[k] for k in "AEFDQCN")

                def out(where, name, dst, fn=ACT.Copy, width=P, **kw):
                    product = where.see(act, step, name)
                    act.activation(dst, product[0:dst.shape[0], 0:width], fn, **kw).then_inc(where.out, 1)

                def scores_out(k, i, dst):
                    out(s, f"{k}_s{i}", dst[:, i * SC:(i + 1) * SC], width=SC, scale=ISQ)

                def gelu_out(where, name, half):
                    product = where.see(act, step, name)
                    for k in range(2 * half, 2 * half + 2):
                        ins = act.activation(hT[:, k, :], product[:, k % 2 * 2 * P:(k % 2 + 1) * 2 * P], ACT.Gelu,
                                             bias=part("bfc")[:, k:k + 1])
                    ins.then_inc(where.out, 1)

                def weights_out(k, i):
                    end = min((i + 1) * TURN, WC)
                    out(t, f"{k}_t{i}", pT[k][:, i * TURN * P:end * P], width=(end - i * TURN) * P)

                def heads_out(k, tile):
                    if tile >= 1:
                        act.wait_ge(on_ready[k], step.done(tile))
                        act.sem_inc(gate, 1)
                    out(o, f"{k}_o", osb[k][:, :], width=H * VW)

                if step.has("E"):
                    weights_out("e", 0)
                    weights_out("e", 1)
                if step.has("C"):
                    act.wait_ge(top_ready, step.done(p + 1, H))
                    if p >= 1:
                        act.wait_ge(p1_ready, step.done(p))
                    act.activation(mask[:, :], rest[p % 2][:, :], ACT.Relu, bias=-0.5, scale=1.0 / TAKEN)\
                       .then_inc(mask_ready, 1)
                if step.has("E"):
                    weights_out("e", 2)
                if step.has("A"):
                    out(m, "a_xT", xT["a"][:, :])
                if step.has("D"):
                    act.wait_ge(hA_ready, step.done(d + 1))
                    act.activation(hq[:, :], hid[:, :], ACT.Copy, scale=hA[:, d % 2:d % 2 + 1], bias=ROUND)\
                       .then_inc(hq_ready, 1)
                if step.has("A"):
                    out(m, "a_q", qT["a"][:, :], ACT.Identity, bias=part("bq0"))
                if step.has("D"):
                    out(g, "d_hT", hqT[:, :], ACT.Copy, width=FF, bias=-ROUND)
                if step.has("C"):
                    act.wait_ge(sm1_ready, step.done(p + 1))
                    act.activation(e1[:, :], sm1[:, :], ACT.Exp).then_inc(e1_ready, 1)
                if step.has("A"):
                    if a >= 1:
                        act.wait_ge(s0_shifted, step.done(a))
                        act.sem_inc(gate, 1)
                    scores_out("a", 0, s0)
                if step.has("E"):
                    heads_out("e", e)
                if step.has("A"):
                    scores_out("a", 1, s0)
                if step.has("N"):
                    out(m, "n_xT", x4T[:, n % 2, :])
                if step.has("A"):
                    scores_out("a", 2, s0)
                    scores_out("a", 3, s0)
                if step.has("E"):
                    out(m, "e_oT", oT["e"][:, :], ACT.Identity, bias=part("bv0"))
                if step.has("C"):
                    weights_out("c", 0)
                if step.has("E"):
                    if e >= 2:
                        u.landed(act, step, "d_down", back=1)
                        act.sem_inc(gate, 1)
                    out(m, "e_out", x1[:, e % 2, :])
                if step.has("G"):
                    gelu_out(g, "g_h0", 0)
                if step.has("C"):
                    weights_out("c", 1)
                if step.has("Q"):
                    out(m, "q_xT", xT["q"][:, :])
                if step.has("G"):
                    gelu_out(u, "g_h1", 1)
                if step.has("Q"):
                    out(m, "q_q", qT["q"][:, :], ACT.Identity, bias=part("bq1"))
                if step.has("C"):
                    weights_out("c", 2)
                if step.has("F"):
                    act.wait_ge(actA_ready, step.done(f + 1))
                    act.activation(yq[:, :], cen["f"][:, f % 2, :], ACT.Copy, scale=actA[:, f % 2:f % 2 + 1], bias=ROUND)\
                       .then_inc(yq_ready, 1)
                if step.has("C"):
                    heads_out("c", p)
                if step.has("F"):
                    out(m, "f_yT", yqT[:, :], ACT.Copy, bias=-ROUND)
                if step.has("Q"):
                    if q >= 2:
                        act.wait_ge(sm1_ready, step.done(q - 1))
                        act.sem_inc(gate, 1)
                    scores_out("q", 0, s1[q % 2])
                if step.has("F"):
                    if f >= 1:
                        act.wait_ge(hid_ready, step.done(f))
                        act.sem_inc(gate, 1)
                    out(g, "f_g", relu_g[:, :], ACT.Relu, width=FF)
                    out(u, "f_u", up_s[:, :], width=FF)
                if step.has("Q"):
                    scores_out("q", 1, s1[q % 2])
                    scores_out("q", 2, s1[q % 2])
                if step.has("C"):
                    out(m, "c_oT", oT["c"][:, :], ACT.Identity, bias=part("bv1"))
                if step.has("Q"):
                    scores_out("q", 3, s1[q % 2])
                if step.has("A"):
                    act.wait_ge(s0_shifted, step.done(a + 1))
                    act.activation(e0[:, :], e0[:, :], ACT.Exp).then_inc(e0_ready, 1)
                if step.has("G"):
                    gg = (c - 3) // 2
                    if gg >= 1:
                        act.wait_ge(y_stored, step.pairs(gg, 16))
                        act.sem_inc(gate, 1)
                    product = u.see(act, step, "g_out")
                    act.activation(y[:, :, :], product[:, 0:2 * D].rearrange("p (i d) -> p i d", i=2), ACT.Copy)\
                       .then_inc(u.out, 1)
                if step.has("C"):
                    out(m, "c_out", x3[:, p % 2, :])

            def keys_out(layer, setup, bias):
                keys = s.see(act, setup, f"keys{layer}")
                act.activation(KT[layer][:, :], keys[:, 0:B * CTX], ACT.Identity, bias=bias).then_inc(s.out, 1)

            def setup_(setup):
                if setup == "setup0":
                    act.wait_ge(pa_in, 16)
                    keys_out(0, setup0, part("bk0"))
                    act.activation(ctx3[:, :].rearrange("p (b r j) -> p b r j", r=3, j=CTX),
                                   part("ctx").rearrange("p (b j) -> p b j", j=CTX).unsqueeze(2)
                                   .to_broadcast([P, B, 3, CTX]), ACT.Copy).then_inc(ctx3_ready, 1)
                    for layer in range(2):
                        act.activation(values_of(layer)[:, :, :, DH],
                                       part("vmask").unsqueeze(1).to_broadcast([P, B, WC * WH]), ACT.Copy)\
                           .then_inc(ctx3_ready, 1)
                if setup == "setup2":
                    keys_out(1, setup2, part("bk1"))
                for b, when in enumerate(VALUES):
                    if when == setup:
                        product = t.see(act, Step(setup), f"v{b}")
                        if b >= 2:
                            act.wait_ge(v_masked, 2 * (b - 1))
                        act.activation(v_raw[:, b % 2, :], product[:, 0:WC * 2 * WH * DH], ACT.Copy).then_inc(t.out, 1)
                        t.landed(act, Step(setup), f"v{b}")
                        act.sem_inc(v_copied, 1)

            all_steps(act, step_, setup_)

        @block.tensor
        def _(pe):
            def keys(layer, setup):
                dst = s.take(pe, setup, f"keys{layer}")
                pe.matmul(dst[:, 0:B * CTX], part(f"wk{layer}"), part("ctx"), start=True, stop=True).then_inc(s.full, 1)

            def values(b, setup):
                dst = t.take(pe, setup, f"v{b}")
                both = pa_s[:, PA["wv0"][0]:PA["wv1"][1]].rearrange("p (l d) -> p l d", l=2)
                for i in range(WC):
                    at = place(i) * 2 * WH * DH
                    tokens = b * REP + start(i) % CTX
                    ins = pe.matmul(dst[:, at:at + 2 * WH * DH], ctx3[:, tokens:tokens + P],
                                    both[:, :, first_head(i) * DH:(first_head(i) + WH) * DH], start=True, stop=True)
                ins.then_inc(t.full, 1)

            def transpose(step, name, src):
                dst = m.take(pe, step, name)
                pe.transpose(dst[:, 0:P], src, ident).then_inc(m.full, 1)

            def project(step, name, k, w):
                dst = m.take(pe, step, name)
                m.landed(pe, step, f"{name[0]}_xT")
                pe.matmul(dst[:, 0:P], part(w), xT[k][:, :], start=True, stop=True).then_inc(m.full, 1)

            def scores(step, k, layer, tile, i):
                dst = s.take(pe, step, f"{k}_s{i}")
                keys = KB[layer][:, bass.ds(step.batch(tile) * HJ + i * SC, SC)]
                pe.matmul(dst[:, 0:SC], qT[k][:, :], keys, start=True, stop=True).then_inc(s.full, 1)

            def turn_weights(step, k, i, src):
                dst = t.take(pe, step, f"{k}_t{i}")
                for n in range(i * TURN, min((i + 1) * TURN, WC)):
                    ins = pe.transpose(dst[:, n % TURN * P:(n % TURN + 1) * P], src[:, start(n):start(n) + P], ident)
                ins.then_inc(t.full, 1)

            def weigh(step, k, layer, tile, i):
                b = step.batch(tile)
                if i == 0 and k == "e" and step.j is None and tile in (0, TPB):
                    pe.wait_ge(v_masked, 2 if tile == 0 else 4)
                dst = o.take(pe, step, f"{k}_o") if i == 0 else o.slot(step, f"{k}_o")
                t.landed(pe, step, f"{k}_t{i}")
                for n in range(i * TURN, min((i + 1) * TURN, WC)):
                    heads_ = (first_head(n), first_head(n) + WH) if n else (0, H)
                    ins = pe.matmul(dst[:, heads_[0] * VW:heads_[1] * VW], pT[k][:, n * P:(n + 1) * P],
                                    V[layer][:, bass.ds(b * VB_W + place(n) * WH * VW, (heads_[1] - heads_[0]) * VW)],
                                    start=(n == 0), stop=(n == WC - 1))
                if i == NT - 1:
                    ins.then_inc(o.full, 1)

            def residual(step, name, k, w, bias, x):
                dst = m.take(pe, step, name)[:, 0:D]
                pe.matmul(dst, oT[k][:, :], part(w), start=True, stop=False)
                pe.matmul(dst, ones[:, :], row(bias), start=False, stop=False)
                pe.matmul(dst, ident, x, start=False, stop=True).then_inc(m.full, 1)

            def hidden(step, where, name, half):
                dst = where.take(pe, step, name)
                for k in range(2 * half, 2 * half + 2):
                    ins = pe.matmul(dst[:, k % 2 * 2 * P:(k % 2 + 1) * 2 * P], fcW[:, k * P:(k + 1) * P],
                                    x4T[:, :, :].rearrange("p i t -> p (i t)"), start=True, stop=True)
                ins.then_inc(where.full, 1)

            def step_(step):
                a, e, f, d, q, p, n = (step.c + AT[k] for k in "AEFDQCN")
                if step.has("E"):
                    pe.wait_ge(e0_ready, step.done(e + 1))
                    turn_weights(step, "e", 0, e0)
                    turn_weights(step, "e", 1, e0)
                    weigh(step, "e", 0, e, 0)
                    turn_weights(step, "e", 2, e0)
                if step.has("A"):
                    pe.wait_ge(ln["a"]["normed"], step.done(a + 1))
                    transpose(step, "a_xT", xn["a"][:, :])
                if step.has("E"):
                    weigh(step, "e", 0, e, 1)
                if step.has("A"):
                    project(step, "a_q", "a", "wq0")
                if step.has("D"):
                    pe.wait_ge(hq_ready, step.done(d + 1))
                    dst = g.take(pe, step, "d_hT")
                    for k in range(FC):
                        ins = pe.transpose(dst[:, k * P:(k + 1) * P], hq[:, k * P:(k + 1) * P], ident)
                    ins.then_inc(g.full, 1)
                if step.has("A"):
                    if a == 0:
                        pe.wait_ge(kb_ready, 1)
                    if step.c == 1:
                        pe.wait_ge(kb_rest, 2)
                    m.landed(pe, step, "a_q")
                    scores(step, "a", 0, a, 0)
                if step.has("E"):
                    weigh(step, "e", 0, e, 2)
                if step.has("D"):
                    dst = u.take(pe, step, "d_down")
                    g.landed(pe, step, "d_hT")
                    for k in range(FC):
                        ins = pe.matmul(dst[:, 0:D], hqT[:, k * P:(k + 1) * P], downQ[:, k * D:(k + 1) * D],
                                        start=(k == 0), stop=(k == FC - 1))
                    ins.then_inc(u.full, 1)
                if step.has("A"):
                    scores(step, "a", 0, a, 1)
                if step.has("N"):
                    pe.wait_ge(ln["n"]["normed"], step.done(n + 1))
                    transpose(step, "n_xT", xn["n"][:, :])
                if step.has("A"):
                    scores(step, "a", 0, a, 2)
                    scores(step, "a", 0, a, 3)
                if step.has("E"):
                    pe.wait_ge(on_ready["e"], step.done(e + 1))
                    transpose(step, "e_oT", on["e"][:, :])
                if step.has("G"):
                    m.landed(pe, step, "n_xT")
                    hidden(step, g, "g_h0", 0)
                if step.has("C"):
                    pe.wait_ge(p1_ready, step.done(p + 1))
                    turn_weights(step, "c", 0, p1)
                if step.has("E"):
                    if e == 0:
                        pe.wait_ge(row_split, 3 * ROW_PARTS + 1)
                    residual(step, "e_out", "e", "wo0", "bo0", xin[:, e % 2, :])
                if step.has("G"):
                    hidden(step, u, "g_h1", 1)
                if step.has("C"):
                    turn_weights(step, "c", 1, p1)
                if step.has("Q"):
                    pe.wait_ge(ln["q"]["normed"], step.done(q + 1))
                    transpose(step, "q_xT", xn["q"][:, :])
                if step.has("C"):
                    weigh(step, "c", 1, p, 0)
                if step.has("Q"):
                    project(step, "q_q", "q", "wq1")
                if step.has("C"):
                    turn_weights(step, "c", 2, p1)
                    weigh(step, "c", 1, p, 1)
                    weigh(step, "c", 1, p, 2)
                if step.has("F"):
                    pe.wait_ge(yq_ready, step.done(f + 1))
                    transpose(step, "f_yT", yq[:, :])
                if step.has("Q"):
                    if q == 0:
                        pe.wait_ge(kb_ready, 2)
                    m.landed(pe, step, "q_q")
                    scores(step, "q", 1, q, 0)
                if step.has("F"):
                    m.landed(pe, step, "f_yT")
                    if f == 0:
                        pe.wait_ge(w_ready, 3)
                    for where, name, w in ((g, "f_g", gateQ), (u, "f_u", upQ)):
                        dst = where.take(pe, step, name)
                        pe.matmul(dst[:, :], yqT[:, :], w[:, :], start=True, stop=True).then_inc(where.full, 1)
                if step.has("Q"):
                    scores(step, "q", 1, q, 1)
                    scores(step, "q", 1, q, 2)
                if step.has("C"):
                    pe.wait_ge(on_ready["c"], step.done(p + 1))
                    transpose(step, "c_oT", on["c"][:, :])
                if step.has("Q"):
                    scores(step, "q", 1, q, 3)
                if step.has("G"):
                    g.landed(pe, step, "g_h0")
                    dst = u.take(pe, step, "g_out")
                    for i in range(2):
                        for k in range(FC):
                            pe.matmul(dst[:, i * D:(i + 1) * D], hT[:, k, i * P:(i + 1) * P], projW[:, k * D:(k + 1) * D],
                                      start=(k == 0), stop=False)
                        pe.matmul(dst[:, i * D:(i + 1) * D], ones[:, :], row("bproj"), start=False, stop=False)
                        ins = pe.matmul(dst[:, i * D:(i + 1) * D], ident, x3[:, i, :], start=False, stop=True)
                    ins.then_inc(u.full, 1)
                if step.has("C"):
                    pe.wait_ge(x2_kept[p % 2], step.loaded(p))
                    residual(step, "c_out", "c", "wo1", "bo1", x2keep[:, p % 2, :])
                if step.c == LOOP[0] - 1:
                    pe.wait_ge(kb_rest, 2 * (B - 1))
                    pe.wait_ge(v_masked, 2 * B)

            def setup_(setup):
                if setup == "setup0":
                    pe.wait_ge(pa_in, 16)
                    pe.wait_ge(consts_set, 1)
                    keys(0, setup0)
                if setup == "setup1":
                    pe.wait_ge(ctx3_ready, 3)
                if setup == "setup2":
                    pe.wait_ge(pc_in, 16)
                    keys(1, setup2)
                for b, when in enumerate(VALUES):
                    if when == setup:
                        values(b, Step(setup))
                if setup == "setup5":
                    pe.wait_ge(r16_in, 16)
                    pe.matmul(g.take(pe, setup5, "lora_fc")[:, :], part("afc"), part("bfcT"), start=True, stop=True)\
                      .then_inc(g.full, 1)
                    dst = u.take(pe, setup5, "lora_proj")
                    for k in range(FC):
                        ins = pe.matmul(dst[:, k * D:(k + 1) * D], part("aproj")[:, k * P:(k + 1) * P], part("bprojT"),
                                        start=True, stop=True)
                    ins.then_inc(u.full, 1)

            all_steps(pe, step_, setup_)

        @block.sync
        def _(sp):
            x_t = x.rearrange("(t p) d -> t p d", p=P)
            out_g = out.rearrange("(g i p) d -> g p i d", i=2, p=P)

            def step_(step):
                c = step.c
                if c >= FIRST + 1:
                    sp.wait_ge(dve_over, step.plus(c - FIRST, 2))
                    sp.sem_inc(gate, 1)
                    sp.wait_ge(dve_step[(c - 1) % 2], dve_counts[standing_for(c - 1)])
                    sp.sem_inc(gate, 1)
                    sp.sem_clear(dve_step[(c - 1) % 2])
                    sp.sem_inc(dve_cleared, 1)
                if step.has("T"):
                    u.landed(sp, step, "d_down", back=1)
                    if c >= 2:
                        sp.sem_inc(gate, 1)
                        m.used(sp, step, "c_out", back=1)
                    sp.dma_start(x2keep[:, c % 2, :], x2[:, c % 2, :]).then_inc(x2_kept[c % 2], 16)
                if step.has("L"):
                    tile = c + AT["L"]
                    if tile >= 2:
                        m.used(sp, step, "e_out")
                    sp.dma_start(xin[:, tile % 2, :], x_t[step.plus(tile, 2)]).then_inc(x_in[tile % 2], 16)
                if step.has("G"):
                    gg = (c - 3) // 2
                    u.landed(sp, step, "g_out")
                    sp.dma_start(out_g[step.pairs(gg, 1)], y[:, :, :]).then_inc(y_stored, 16)

            sp.dma_start(xin[:, 0, :], x_t[0]).then_inc(x_in[0], 16)
            sp.dma_start(pa_s[:, :], pa).then_inc(pa_in, 16)
            sp.dma_start(row_s[:, :], rows).then_inc(row_in, 16)

            def setup_(setup):
                if setup == "setup1":
                    sp.dma_start(pb_s[:, :], pb).then_inc(pb_in, 16)
                    sp.dma_start(pc_s[:, :], pc).then_inc(pc_in, 16)
                    sp.dma_start(r16_s[:, :], r16).then_inc(r16_in, 16)

            all_steps(sp, step_, setup_)
            sp.wait_ge(y_stored, 16 * (TILES // 2))


DUE = {"a_stats": 0, "d_hidden": 2, "n_stats": 12, "d_residual": 36, "e_recip": 38,
       "a_max": 50, "f_stats": 66, "f_scale": 76, "c_recip": 94}


def kernel(x, ctx_1024, **w):
    import numpy as np
    import concourse.bacc as bacc
    from concourse.bass_utils import run_bass_kernel_spmd

    w = {k: np.asarray(v) for k, v in w.items()}
    x, ctx_1024 = np.asarray(x), np.asarray(ctx_1024)

    def col(v):
        return v.reshape(-1, P).T

    def chunked(v):
        return v.T.reshape(FC, P, D).transpose(1, 0, 2).reshape(P, FF)

    dt = x.dtype
    ident = np.eye(P, dtype=dt)
    hmask = np.repeat(np.eye(H, dtype=dt), DH, axis=0)
    ctxT = ctx_1024.reshape(B * CTX, D).T
    vmask = np.zeros((P, WC, WH), dt)
    for i in range(WC):
        for r in range(P):
            head = (start(i) + r) // CTX - first_head(i)
            if start(i) + r >= i * P:
                vmask[r, place(i), head] = 1
    pa = np.concatenate([ident, hmask, col(w["L0_xattn_b_q"]), col(w["L0_xattn_b_k"]), col(w["L0_xattn_b_v"]),
                         vmask.reshape(P, WC * WH), w["L0_xattn_w_q"].T,
                         w["L0_xattn_w_k"].T, w["L0_xattn_w_v"].T, w["L1_xattn_Wv"].T, w["L0_xattn_w_o"].T, ctxT], axis=1)
    pb = np.concatenate([w["L0_ffn_w_gate"].T, w["L0_ffn_w_up"].T, chunked(w["L0_ffn_w_down"])], axis=1)
    pc = np.concatenate([w["L1_xattn_Wq"].T, w["L1_xattn_Wk"].T, w["L1_xattn_Wo"].T,
                         col(w["L1_xattn_bq"]), col(w["L1_xattn_bk"]), col(w["L1_xattn_bv"]), col(w["L1_ffn_b_fc"]), w["L1_ffn_W_fc"].T,
                         chunked(w["L1_ffn_W_proj"])], axis=1)
    rows = np.concatenate([w["L0_xattn_b_o"], w["L1_xattn_bo"],
                           w["L1_ffn_b_proj"]])[None, :].repeat(ROW_PARTS, axis=0)
    r16 = np.concatenate([w["L1_ffn_A_fc"], w["L1_ffn_B_fc"].T, w["L1_ffn_A_proj"], w["L1_ffn_B_proj"].T], axis=1)
    arrays = {"x": x.reshape(B * S, D), "pa": pa, "pb": pb, "pc": pc, "rows": rows, "r16": r16}
    arrays = {f"in_{k}": np.ascontiguousarray(v) for k, v in arrays.items()}

    nc = bacc.Bacc("TRN2", target_bir_lowering=False, num_devices=1)
    args = [nc.dram_tensor(k, v.shape, mybir.dt.from_np(v.dtype), kind="ExternalInput").ap() for k, v in arrays.items()]
    out = nc.dram_tensor("out_y", (B * S, D), F32, kind="ExternalOutput").ap()
    build(nc, *args, out)
    r = run_bass_kernel_spmd(nc, [arrays], core_ids=[0])
    return r.results[0]["out_y"].reshape(B, S, D)
```
